# Optimizing a Trainium2 kernel written in Bass

```python
import numpy as np
import jax
import jax.numpy as jnp

def _softmax(x, axis=-1):
    return jax.nn.softmax(x, axis=axis)

def _gelu(x):
    return jax.nn.gelu(x, approximate=True)

def _silu(x):
    return jax.nn.silu(x)

def _sigmoid(x):
    return jax.nn.sigmoid(x)

def _layernorm(x, axis=-1, eps=1e-05):
    m = jnp.mean(x, axis=axis, keepdims=True)
    v = jnp.var(x, axis=axis, keepdims=True)
    return (x - m) / jnp.sqrt(v + eps)

def _scatter_add(tgt, idx, src, axis=0):
    return tgt.at[idx].add(src)

def _segment_sum(src, seg, n):
    return jax.ops.segment_sum(src, seg, n)
kernel_name = 'mk_early_fusion_d1_tok_img256_r4_ac461f'

def setup_inputs(seed: int=0):
    np.random.seed(seed)
    _w = jnp.asarray

    def _rec_inputs():
        import jax
        import jax.numpy as jnp
        _rk = jax.random.key(seed)
        x = -7.10856e-05 + 0.999911 * jax.random.normal(jax.random.fold_in(_rk, 1), (4, 64, 128, 64), jnp.float32)
        txt = -0.000161634 + 0.479995 * jax.random.normal(jax.random.fold_in(_rk, 2), (4, 512, 64), jnp.float32)
        return (x, txt)
    x, txt = _rec_inputs()

    def _L0_tok_setup():
        import jax, jax.numpy as jnp
        import numpy as np
        PATCH_LEN = 16
        STRIDE = 8
        PAD = 8
        key = jax.random.key(seed)
        k1, k2 = jax.random.split(key)
        x = jax.random.normal(k1, (32, 64, 128, 64), dtype=jnp.float32)
        in_feat = 64 * (PATCH_LEN // 2 + 1) * 2
        W = jax.random.normal(k2, (64, in_feat), dtype=jnp.float32) * 0.02
        return {'x': x, 'W': W}
    _L0_tok_all = _L0_tok_setup()
    _L0_tok_in = {k: v for k, v in _L0_tok_all.items() if k in ('W',)}
    del _L0_tok_all

    def _L0_attn_setup():
        import jax, jax.numpy as jnp
        import numpy as np
        NUM_HEADS = 4
        LN_EPS = 1e-05

        def positional_encoding(length, d_model):
            pos = jnp.arange(length, dtype=jnp.float32)[:, None]
            div = jnp.exp(jnp.arange(0, d_model, 2, dtype=jnp.float32) * (-np.log(10000.0) / d_model))
            pe = jnp.zeros((length, d_model), dtype=jnp.float32)
            pe = pe.at[:, 0::2].set(jnp.sin(pos * div))
            pe = pe.at[:, 1::2].set(jnp.cos(pos * div))
            return pe

        def rel_shift(pos_score):
            B, H, S, _ = pos_score.shape
            padded = jnp.pad(pos_score, ((0, 0), (0, 0), (0, 0), (1, 0)))
            padded = padded.reshape(B, H, S + 1, S)
            return padded[:, :, 1:].reshape(B, H, S, S)
        key = jax.random.key(seed)
        ks = jax.random.split(key, 8)
        B, S, D, H = (8, 512, 64, NUM_HEADS)
        dh = D // H
        s = 0.02
        return {'inputs': jax.random.normal(ks[0], (B, S, D), dtype=jnp.float32), 'ln_gamma': jnp.ones((D,), jnp.float32), 'ln_beta': jnp.zeros((D,), jnp.float32), 'Wq': jax.random.normal(ks[1], (D, D), jnp.float32) * s, 'bq': jnp.zeros((D,), jnp.float32), 'Wk': jax.random.normal(ks[2], (D, D), jnp.float32) * s, 'bk': jnp.zeros((D,), jnp.float32), 'Wv': jax.random.normal(ks[3], (D, D), jnp.float32) * s, 'bv': jnp.zeros((D,), jnp.float32), 'Wpos': jax.random.normal(ks[4], (D, D), jnp.float32) * s, 'u_bias': jax.random.normal(ks[5], (H, dh), jnp.float32) * s, 'v_bias': jax.random.normal(ks[6], (H, dh), jnp.float32) * s, 'Wout': jax.random.normal(ks[7], (D, D), jnp.float32) * s, 'bout': jnp.zeros((D,), jnp.float32)}
    _L0_attn_all = _L0_attn_setup()
    _L0_attn_in = {k: v for k, v in _L0_attn_all.items() if k in ('ln_gamma', 'ln_beta', 'Wq', 'bq', 'Wk', 'bk', 'Wv', 'bv', 'Wpos', 'u_bias', 'v_bias', 'Wout', 'bout')}
    del _L0_attn_all

    def _L0_ffn_setup():
        import jax, jax.numpy as jnp
        import numpy as np
        DIM = 64
        HEADS = 8
        NUM_KEYS = 64
        NUM_KV = NUM_KEYS ** 2
        PK_TOPK = 16
        FINAL_TOPK = 16
        DIM_KEY = DIM // 2
        P = 2

        def _pk(x, Wq_pk, pk_keys):
            b, n, _ = x.shape
            q = (x @ Wq_pk).reshape(b, n, P, HEADS, DIM_KEY).transpose(2, 0, 1, 3, 4)
            sim = jnp.einsum('pbnhd,pkhd->pbnhk', q, pk_keys)
            scores, idx = jax.lax.top_k(sim, PK_TOPK)
            idx0 = idx[0]
            idx1 = idx[1] * NUM_KEYS
            index = (idx0[..., :, None] + idx1[..., None, :]).reshape(b, n, HEADS, PK_TOPK * PK_TOPK)
            score = (scores[0][..., :, None] + scores[1][..., None, :]).reshape(b, n, HEADS, PK_TOPK * PK_TOPK)
            final_scores, pk_idx = jax.lax.top_k(score, FINAL_TOPK)
            final_indices = jnp.take_along_axis(index, pk_idx, axis=-1)
            final_scores = jax.nn.softmax(final_scores, axis=-1)
            return (final_scores, final_indices)
        key = jax.random.key(seed)
        ks = jax.random.split(key, 7)
        b, n = (2, 256)
        std = 0.02
        x = jax.random.normal(ks[0], (b, n, DIM), dtype=jnp.float32)
        Wq_pk = jax.random.normal(ks[1], (DIM, P * HEADS * DIM_KEY), dtype=jnp.float32) * std
        pk_keys = jax.random.normal(ks[2], (P, NUM_KEYS, HEADS, DIM_KEY), dtype=jnp.float32) * std
        Wq = jax.random.normal(ks[3], (DIM, HEADS * DIM), dtype=jnp.float32) * std
        keys_table = jax.random.normal(ks[4], (NUM_KV * HEADS, DIM), dtype=jnp.float32) * std
        values_table = jax.random.normal(ks[5], (NUM_KV * HEADS, DIM), dtype=jnp.float32) * std
        Wo = jax.random.normal(ks[6], (DIM * HEADS, DIM), dtype=jnp.float32) * std
        return {'x': x, 'Wq_pk': Wq_pk, 'pk_keys': pk_keys, 'Wq': Wq, 'keys_table': keys_table, 'values_table': values_table, 'Wo': Wo}
    _L0_ffn_all = _L0_ffn_setup()
    _L0_ffn_in = {k: v for k, v in _L0_ffn_all.items() if k in ('Wq_pk', 'pk_keys', 'Wq', 'keys_table', 'values_table', 'Wo')}
    del _L0_ffn_all
    return {'x': x, 'txt': txt, 'L0_tok_W': _L0_tok_in['W'], 'L0_attn_ln_gamma': _L0_attn_in['ln_gamma'], 'L0_attn_ln_beta': _L0_attn_in['ln_beta'], 'L0_attn_Wq': _L0_attn_in['Wq'], 'L0_attn_bq': _L0_attn_in['bq'], 'L0_attn_Wk': _L0_attn_in['Wk'], 'L0_attn_bk': _L0_attn_in['bk'], 'L0_attn_Wv': _L0_attn_in['Wv'], 'L0_attn_bv': _L0_attn_in['bv'], 'L0_attn_Wpos': _L0_attn_in['Wpos'], 'L0_attn_u_bias': _L0_attn_in['u_bias'], 'L0_attn_v_bias': _L0_attn_in['v_bias'], 'L0_attn_Wout': _L0_attn_in['Wout'], 'L0_attn_bout': _L0_attn_in['bout'], 'L0_ffn_Wq_pk': _L0_ffn_in['Wq_pk'], 'L0_ffn_pk_keys': _L0_ffn_in['pk_keys'], 'L0_ffn_Wq': _L0_ffn_in['Wq'], 'L0_ffn_keys_table': _L0_ffn_in['keys_table'], 'L0_ffn_values_table': _L0_ffn_in['values_table'], 'L0_ffn_Wo': _L0_ffn_in['Wo']}

def reference(x, txt, L0_tok_W, L0_attn_ln_gamma, L0_attn_ln_beta, L0_attn_Wq, L0_attn_bq, L0_attn_Wk, L0_attn_bk, L0_attn_Wv, L0_attn_bv, L0_attn_Wpos, L0_attn_u_bias, L0_attn_v_bias, L0_attn_Wout, L0_attn_bout, L0_ffn_Wq_pk, L0_ffn_pk_keys, L0_ffn_Wq, L0_ffn_keys_table, L0_ffn_values_table, L0_ffn_Wo):
    import jax
    import jax.numpy as jnp

    def _L0_tok_ref(x, W):
        import jax, jax.numpy as jnp
        import numpy as np
        PATCH_LEN = 16
        STRIDE = 8
        PAD = 8
        B, C, T, V = x.shape
        xp = jnp.pad(x, ((0, 0), (0, 0), (0, PAD), (0, 0)), mode='edge')
        Tp = T + PAD
        N = (Tp - PATCH_LEN) // STRIDE + 1
        idx = jnp.arange(N)[:, None] * STRIDE + jnp.arange(PATCH_LEN)[None, :]
        patches = xp[:, :, idx, :]
        patches = jnp.transpose(patches, (0, 4, 2, 3, 1))
        xf = jnp.fft.rfft(patches, axis=-2, norm='ortho')
        F = xf.shape[-2]
        x_real = xf.real.reshape(B, V, N, F * C)
        x_imag = xf.imag.reshape(B, V, N, F * C)
        x_emb = jnp.concatenate([x_real, x_imag], axis=-1)
        x_emb = x_emb @ W.T
        return x_emb.reshape(B, V * N, -1)

    def _L0_attn_ref(inputs, ln_gamma, ln_beta, Wq, bq, Wk, bk, Wv, bv, Wpos, u_bias, v_bias, Wout, bout):
        import jax, jax.numpy as jnp
        import numpy as np
        NUM_HEADS = 4
        LN_EPS = 1e-05

        def positional_encoding(length, d_model):
            pos = jnp.arange(length, dtype=jnp.float32)[:, None]
            div = jnp.exp(jnp.arange(0, d_model, 2, dtype=jnp.float32) * (-np.log(10000.0) / d_model))
            pe = jnp.zeros((length, d_model), dtype=jnp.float32)
            pe = pe.at[:, 0::2].set(jnp.sin(pos * div))
            pe = pe.at[:, 1::2].set(jnp.cos(pos * div))
            return pe

        def rel_shift(pos_score):
            B, H, S, _ = pos_score.shape
            padded = jnp.pad(pos_score, ((0, 0), (0, 0), (0, 0), (1, 0)))
            padded = padded.reshape(B, H, S + 1, S)
            return padded[:, :, 1:].reshape(B, H, S, S)
        B, S, D = inputs.shape
        H = NUM_HEADS
        dh = D // H
        mu = jnp.mean(inputs, axis=-1, keepdims=True)
        var = jnp.mean(jnp.square(inputs - mu), axis=-1, keepdims=True)
        x = (inputs - mu) / jnp.sqrt(var + LN_EPS) * ln_gamma + ln_beta
        pe = positional_encoding(S, D)
        q = (x @ Wq + bq).reshape(B, S, H, dh)
        k = (x @ Wk + bk).reshape(B, S, H, dh)
        v = (x @ Wv + bv).reshape(B, S, H, dh)
        p = (pe @ Wpos).reshape(S, H, dh)
        content_score = jnp.einsum('bshd,bthd->bhst', q + u_bias, k)
        pos_score = jnp.einsum('bshd,thd->bhst', q + v_bias, p)
        pos_score = rel_shift(pos_score)
        score = (content_score + pos_score) / np.sqrt(D).astype(np.float32)
        attn = jax.nn.softmax(score, axis=-1)
        ctx = jnp.einsum('bhst,bthd->bshd', attn, v).reshape(B, S, D)
        return ctx @ Wout + bout

    def _L0_ffn_ref(x, Wq_pk, pk_keys, Wq, keys_table, values_table, Wo):
        import jax, jax.numpy as jnp
        import numpy as np
        DIM = 64
        HEADS = 8
        NUM_KEYS = 64
        NUM_KV = NUM_KEYS ** 2
        PK_TOPK = 16
        FINAL_TOPK = 16
        DIM_KEY = DIM // 2
        P = 2

        def _pk(x, Wq_pk, pk_keys):
            b, n, _ = x.shape
            q = (x @ Wq_pk).reshape(b, n, P, HEADS, DIM_KEY).transpose(2, 0, 1, 3, 4)
            sim = jnp.einsum('pbnhd,pkhd->pbnhk', q, pk_keys)
            scores, idx = jax.lax.top_k(sim, PK_TOPK)
            idx0 = idx[0]
            idx1 = idx[1] * NUM_KEYS
            index = (idx0[..., :, None] + idx1[..., None, :]).reshape(b, n, HEADS, PK_TOPK * PK_TOPK)
            score = (scores[0][..., :, None] + scores[1][..., None, :]).reshape(b, n, HEADS, PK_TOPK * PK_TOPK)
            final_scores, pk_idx = jax.lax.top_k(score, FINAL_TOPK)
            final_indices = jnp.take_along_axis(index, pk_idx, axis=-1)
            final_scores = jax.nn.softmax(final_scores, axis=-1)
            return (final_scores, final_indices)
        b, n, d = x.shape
        q = (x @ Wq).reshape(b, n, HEADS, DIM) * DIM ** (-0.5)
        kv_scores, indices = _pk(x, Wq_pk, pk_keys)
        offsets = jnp.arange(HEADS, dtype=indices.dtype) * NUM_KV
        ind = indices + offsets[None, None, :, None]
        k = jnp.einsum('bnhk,bnhkd->bnhd', kv_scores, keys_table[ind])
        v = jnp.einsum('bnhk,bnhkd->bnhd', kv_scores, values_table[ind])
        sim = jnp.einsum('bihd,bjhd->bhij', q, k)
        neg = -jnp.finfo(sim.dtype).max
        causal = jnp.tril(jnp.ones((n, n), dtype=bool))
        sim = jnp.where(causal, sim, neg)
        attn = jax.nn.softmax(sim, axis=-1)
        out = jnp.einsum('bhij,bjhd->bhid', attn, v)
        out = out.transpose(0, 2, 1, 3).reshape(b, n, HEADS * DIM)
        return out @ Wo
    h = _L0_tok_ref(x, L0_tok_W)
    h = jnp.concatenate([h, txt], axis=1)
    h = h + _L0_attn_ref(_layernorm(h, axis=-1), L0_attn_ln_gamma, L0_attn_ln_beta, L0_attn_Wq, L0_attn_bq, L0_attn_Wk, L0_attn_bk, L0_attn_Wv, L0_attn_bv, L0_attn_Wpos, L0_attn_u_bias, L0_attn_v_bias, L0_attn_Wout, L0_attn_bout)
    h = h + _L0_ffn_ref(_layernorm(h, axis=-1), L0_ffn_Wq_pk, L0_ffn_pk_keys, L0_ffn_Wq, L0_ffn_keys_table, L0_ffn_values_table, L0_ffn_Wo)
    return h

_drawn_inputs = setup_inputs


def setup_inputs(seed=0):
    import zlib

    import numpy as np

    out = dict(_drawn_inputs(seed))
    spreads = {'L0_attn_ln_gamma': (1.0, 0.6),
     'L0_attn_ln_beta': (0.0, 0.8),
     'L0_attn_bq': (0.0, 0.8),
     'L0_attn_bk': (0.0, 2.0),
     'L0_attn_bv': (0.0, 0.1),
     'L0_attn_bout': (0.0, 0.1)}
    factors = {'L0_attn_Wq': 8.0,
     'L0_attn_Wk': 8.0,
     'L0_attn_Wv': 8.0,
     'L0_attn_Wpos': 8.0,
     'L0_attn_u_bias': 8.0,
     'L0_attn_v_bias': 61.35,
     'L0_ffn_Wq_pk': 8.0,
     'L0_ffn_pk_keys': 8.0,
     'L0_ffn_Wq': 64.0,
     'L0_ffn_keys_table': 64.0,
     'L0_ffn_values_table': 8.0,
     'L0_ffn_Wo': 8.0}
    for name, (base, spread) in spreads.items():
        noise = np.random.default_rng([zlib.crc32(name.encode()), seed]).standard_normal(out[name].shape)
        drawn = base * np.exp(spread * noise) if base else spread * noise
        out[name] = jnp.asarray(drawn.astype(out[name].dtype))
    for name, factor in factors.items():
        out[name] = (out[name] * factor).astype(out[name].dtype)
    return out
```

```python
from contextlib import ExitStack

import numpy as np

import concourse.bass as bass
from concourse import mybir

F32 = mybir.dt.float32
U32 = mybir.dt.uint32
I32 = mybir.dt.int32
ALU = mybir.AluOpType
ACT = mybir.ActivationFunctionType
AX = mybir.AxisListType

P = 128
B, C, T, V = 4, 64, 128, 64
PATCH, STRIDE = 16, 8
NPATCH = (T + STRIDE - PATCH) // STRIDE + 1
FREQ = PATCH // 2 + 1
D = 64
TXT = 512
S = V * NPATCH + TXT
NT = S // P
NTOK = V * NPATCH // P
H1, DH1 = 4, 16
H2, DH2 = 8, 64
NKEY, TOPK, DKEY = 64, 16, 32
NKV = NKEY * NKEY
EPS = 1e-5
LOWEST = -3.0e38
BANK = 512

SPANS = [(r0, TOPK // (r0 + 1)) for r0 in range(TOPK)]
NCAND = sum(n for _, n in SPANS)
RING = 4


def shape_constants():
    div = np.exp(np.arange(0, D, 2, dtype=np.float32) * np.float32(-np.log(10000.0) / D)).astype(np.float64)
    pos = np.arange(S, dtype=np.float64)
    ang = div[:, None] * pos[None, :]
    pe = np.concatenate([np.sin(ang), np.cos(ang)], 0).astype(np.float32)
    lo = div[:, None] * (S - 1 - pos)[None, :]
    up = div[:, None] * (-(pos + 2))[None, :]
    root = np.sqrt(float(D))
    rot = np.stack([np.concatenate([f, g], 0) / root for a in (lo, up)
                    for f, g in ((np.cos(a), np.cos(a)), (-np.sin(a), np.sin(a)))], 1).astype(np.float32)
    rot = np.ascontiguousarray(rot.reshape(D, 4, NT, P).transpose(2, 0, 1, 3))
    i, j = np.arange(P)[:, None], np.arange(P + 1)[None, :]
    upper = (j[:, :P] >= i + 2).astype(np.int32)
    seam = (j == i + 1).astype(np.int32)
    future = np.where(j[:, :P] > i, np.float32(LOWEST), np.float32(0)).astype(np.float32)
    own = np.zeros((P, 3, H1), np.float32)
    for h in range(H1):
        own[D + h * DH1:D + (h + 1) * DH1, :, h] = 1.0 / root
    iota = np.tile(np.arange(NCAND, dtype=np.float32), (P, 1))
    offs = np.tile(np.repeat(np.arange(H2, dtype=np.float32) * NKV, TOPK), (P, 1))
    p, f = np.arange(PATCH)[None, :], np.arange(FREQ)[:, None]
    t = 2 * np.pi * f * p / PATCH
    dft = (np.concatenate([np.cos(t), -np.sin(t)], 0) / np.sqrt(float(PATCH))).astype(np.float32)
    return {"c_pe": pe, "c_rot": rot, "c_upper": upper, "c_seam": seam, "c_future": future,
            "c_own": own.reshape(P, 3 * H1), "c_iota": iota, "c_offs": offs, "c_dft": dft,
            "c_ident": np.eye(P, dtype=np.float32)}


def plan():
    score, unit, group, misc, output = {}, {}, {}, {}, {}
    groups = 0

    def take(d, key):
        d[key] = len(d)

    def attend(kind, t, h, tiles):
        nonlocal groups
        take(score, (kind, t, h))
        take(unit, (kind, t, h))
        take(output, (kind, t, h))
        group[kind, t, h] = groups
        groups += -(-tiles // 4)

    def relative(t):
        take(misc, ("q", t))
        take(score, ("rot", t))
        for h in range(H1):
            attend("rel", t, h, NT)
        take(output, ("rel_out", t))
        for name in ("ctxT", "xT", "qT", "pkT"):
            take(misc, (name, t))
        take(score, ("sim", t))

    relative(0)
    for t in range(NT):
        if t + 1 < NT:
            relative(t + 1)
        for pair in range(H2 // 2):
            take(misc, ("kT", t, pair))
            for h in (2 * pair, 2 * pair + 1):
                attend("pk", t, h, t + 1)
        take(misc, ("oT", t))
        take(output, ("pk_out", t))
    assert len(unit) % 2 == 0 and groups % 2 == 0
    return score, unit, group, misc, output, groups


def program(nc, a, out):
    score_no, unit_no, group_no, misc_no, output_no, GROUPS = plan()
    SCORES, UNITS, MISCS, OUTPUTS = len(score_no), len(unit_no), len(misc_no), len(output_no)

    with ExitStack() as ctx:
        def sb(name, shape, dt=F32):
            return ctx.enter_context(nc.sbuf_tensor(name, shape, dt))

        def sem(name):
            return ctx.enter_context(nc.semaphore(name))

        ps = ctx.enter_context(nc.psum_tensor("ps", [P, 8 * BANK], F32))
        S_ps = ps[:, 0:4 * BANK]
        X_ps = ps[:, 3 * BANK:4 * BANK]
        T_ps = [ps[:, (4 + i) * BANK:(5 + i) * BANK] for i in range(2)]
        O_ps = ps[:, 6 * BANK:7 * BANK]
        M_ps = ps[:, 7 * BANK:8 * BANK]
        REL_OUT, PK_OUT = O_ps[:, 192:256], O_ps[:, 256:320]

        kfeat = sb("kfeat", [P, B * S])
        xt = [sb(f"xt{i}", [D, P + 1]) for i in range(2)]
        h0 = sb("h0", [P, B * NT, D])
        v1 = sb("v1", [P, B * NT, D])
        kT = sb("kT", [P, H2 // 2, S])
        v2 = sb("v2", [P, NT, H2, DH2])
        union = sb("union", [P, 16384])
        xin = [union[:, i * T * V:(i + 1) * T * V] for i in range(2)]
        rows = [union[:, r * 2048:(r + 1) * 2048].rearrange("p (s d) -> p s d", s=TOPK) for r in range(RING)]
        work = union[:, 8192:8192 + 4 * S]
        probs = [work[:, i * S:(i + 1) * S] for i in range(2)]
        probsT = [work[:, (2 + i) * S:(3 + i) * S] for i in range(2)]
        rot_prod = work[0:D, 0:2048]
        sim = work[:, 0:1024].rearrange("p (l k) -> p l k", k=NKEY)
        sim_rest = work[:, 1024:2048].rearrange("p (l k) -> p l k", k=NKEY)
        match = work[:, 2048:2048 + 4 * TOPK * NCAND]
        cand_rest = work[:, 5248:5648].rearrange("p (h c) -> p h c", h=H2)
        cand_i = work[:, 5648:6048].rearrange("p (h c) -> p h c", h=H2)
        qfeat = union[:, 14336:15872]

        wq2 = sb("wq2", [D, P]); wk2 = sb("wk2", [D, P]); wv = sb("wv", [D, D]); wout = sb("wout", [D, D])
        wpos = sb("wpos", [D, 2, H1, D])
        bq2 = sb("bq2", [P, 1]); uv2 = sb("uv2", [P, 1]); bk2 = sb("bk2", [P, 1]); bquv = sb("bquv", [P, 1])
        bv = sb("bv", [P, D]); bout = sb("bout", [P, D]); gamma = sb("gamma", [P, D]); beta = sb("beta", [P, D])
        wqf = sb("wqf", [D, H2 * DH2]); wpk = sb("wpk", [D, 2 * H2 * DKEY]); wo = sb("wo", [P, H2 // 2, D])
        keys = sb("keys", [P, 4, 4 * NKEY])
        ident = sb("ident", [P, P]); rot = [sb(f"rot{i}", [D, 4, P]) for i in range(2)]
        upper = sb("upper", [P, P], I32); seam = sb("seam", [P, P + 1], I32); future = sb("future", [P, P])
        own = sb("own", [P, 3 * H1]); iota = sb("iota", [P, NCAND]); offs = sb("offs", [P, H2 * TOPK])
        dft = sb("dft", [2 * FREQ, PATCH]); wtok = sb("wtok", [P, PATCH // 2, D])
        w18 = kT[0:2 * FREQ, 0:3, :].rearrange("p a b -> p (a b)")[:, 0:C * D]
        wtok_p = v2[0:PATCH, :, :, :].rearrange("p a b c -> p (a b c)")[:, 0:C * D]

        ln_n = kT[:, 0, 0:768].rearrange("p (t d) -> p t d", t=NT)
        ln_q = kT[:, 1, 0:768].rearrange("p (t d) -> p t d", t=NT)
        xTs = kT[0:D, 2, :]
        embT = kT[0:D, 3, 0:NTOK * P]
        stat = sb("stat", [P, 6, NT])
        tl_n = sb("tl_n", [P, 1, D]); tl_q = sb("tl_q", [P, 1, D])
        qq = sb("qq", [P, P + 1])
        rowmax = sb("rowmax", [P, 2]); rowsum = sb("rowsum", [P, 2]); rowinv = sb("rowinv", [P, 2])
        ctx1 = sb("ctx1", [P, D]); ctxT = sb("ctxT", [D, P]); x2T = sb("x2T", [D, P])
        h1 = [sb(f"h1{i}", [P, D]) for i in range(2)]
        q2T = [sb(f"q2T{i}", [P, 4, P]) for i in range(2)]
        pkT = union[:, 15872:16384].rearrange("p (a b) -> p a b", a=4)
        best = sb("best", [P, 16, TOPK]); best_i = sb("best_i", [P, 16, TOPK], U32)
        i1s = sb("i1s", [P, H2, TOPK])
        cand = sb("cand", [P, H2, NCAND])
        fin = sb("fin", [P, H2, TOPK]); fin_pos = sb("fin_pos", [P, H2, TOPK], U32)
        picked = sb("picked", [P, 4 * TOPK])
        fsum = sb("fsum", [P, H2])
        weight = [sb(f"weight{i}", [P, H2, TOPK]) for i in range(2)]
        index = [sb(f"index{i}", [P, H2 * TOPK], U32) for i in range(2)]
        k2 = sb("k2", [P, H2 // 2, 2 * DH2])
        ao = sb("ao", [P, H2 * DH2]); aoT = sb("aoT", [P, 4, P])
        outt = [sb(f"outt{i}", [P, D]) for i in range(2)]

        weights_in = sem("weights_in"); consts_set = sem("consts_set")
        wtok_made = sem("wtok_made"); wtok_out = sem("wtok_out"); wtok_in = sem("wtok_in"); w18_used = sem("w18_used")
        bias_made = sem("bias_made")
        x_in = [sem(f"x_in{i}") for i in range(2)]; emb_made = sem("emb_made"); emb_kept = sem("emb_kept"); tok_made = sem("tok_made"); tok_kept = sem("tok_kept")
        ln_made = sem("ln_made"); xT_made = sem("xT_made"); xT_kept = sem("xT_kept"); xT_stored = sem("xT_stored")
        pad_stored = sem("pad_stored"); xTs_free = sem("xTs_free"); k_made = sem("k_made"); k_kept = sem("k_kept"); v_made = sem("v_made"); v_kept = sem("v_kept")
        var_ready = sem("var_ready"); dev_ready = sem("dev_ready")
        scores_ready = sem("scores_ready")
        scores_free = sem("scores_free")
        max_ready = sem("max_ready")
        turned = sem("turned")
        turned_kept = sem("turned_kept")
        pv_ready = sem("pv_ready")
        misc_ready = sem("misc_ready")
        misc_kept = sem("misc_kept")
        feat_ready = sem("feat_ready")
        rot_in = [sem(f"rot_in{i}") for i in range(2)]; xt_in = [sem(f"xt_in{i}") for i in range(2)]
        output_free = sem("output_free")
        rel_out = sem("rel_out"); x2_ready = sem("x2_ready")
        exp_asked = sem("exp_asked"); exp_made = sem("exp_made")
        index_ready = sem("index_ready")
        gathered = [sem(f"gathered{i}") for i in range(RING)]
        rows_free = sem("rows_free")
        k2_ready = sem("k2_ready"); pk_out = sem("pk_out")
        out_done = [sem(f"out_done{i}") for i in range(2)]

        xT_dram = nc.dram_tensor("xT_scratch", (D, B * S + 1), F32, kind="Internal").ap()
        scratch = nc.dram_tensor("wtok_scratch", (PATCH, C, D), F32, kind="Internal").ap()
        small = [(wq2, "wq2"), (wk2, "wk2"), (wv, "wv"), (wout, "wout"), (wpos, "wpos"), (wqf, "wqf"), (wpk, "wpk"),
                 (bq2, "bq2"), (uv2, "uv2"), (bk2, "bk2"), (ident, "c_ident"), (upper, "c_upper"),
                 (seam, "c_seam"), (future, "c_future"), (own, "c_own"), (iota, "c_iota"), (offs, "c_offs"),
                 (dft, "c_dft")]
        rowwise = [(bv, "bv"), (bout, "bout"), (gamma, "gamma"), (beta, "beta")]
        N_LOADS = 1 + len(small) + len(rowwise) + 1 + 2 * B + 4

        passed = sem("passed")

        def stand(eng):
            eng.sem_inc(passed, 1)

        block = ctx.enter_context(nc.Block())

        @block.sync
        def _(sp):
            for s in out_done:
                sp.sem_inc(s, 16)
            sp.dma_start(w18, a["w18"]).then_inc(weights_in, 16)
            for dst, name in small:
                sp.dma_start(dst[:], a[name]).then_inc(weights_in, 16)
            for dst, name in rowwise:
                sp.dma_start(dst[:], a[name].partition_broadcast(P)).then_inc(weights_in, 16)
            sp.dma_start(wo[:], a["wo"].rearrange("(q p) d -> p q d", p=P)).then_inc(weights_in, 16)
            for b in range(B):
                sp.dma_start(kfeat[0:D, b * S:(b + 1) * S], a["c_pe"]).then_inc(weights_in, 16)
                sp.dma_start(h0[:, b * NT + NTOK:(b + 1) * NT, :],
                             a["txt"][b].rearrange("(t p) d -> p t d", p=P)).then_inc(weights_in, 16)
            sp.wait_ge(consts_set, 1)
            for q in range(4):
                sp.dma_start(keys[q * DKEY:(q + 1) * DKEY, :, q * NKEY:(q + 1) * NKEY],
                             a["keys"][:, q].rearrange("l d k -> d l k")).then_inc(weights_in, 16)
            sp.wait_ge(wtok_made, 1)
            sp.dma_start(scratch.rearrange("p c d -> p (c d)"), wtok_p).then_inc(wtok_out, 16)
            sp.wait_ge(wtok_out, 16)
            for half in range(2):
                sp.dma_start(wtok[half * C:(half + 1) * C, :, :],
                             scratch[half * 8:(half + 1) * 8].rearrange("p c d -> c p d")).then_inc(wtok_in, 16)
            with sp.Fori(0, B // 2) as i:
                for par in range(2):
                    sp.wait_ge(tok_made, i * 2 + par + 1)
                    x = a["x"][bass.ds(i * 2 + par, 1)].rearrange("b c t v -> (b c) (t v)")
                    sp.dma_start(xin[par][0:C, :], x).then_inc(x_in[par], 16)
                    sp.dma_start(xin[par][C:2 * C, 0:(T - STRIDE) * V], x[:, STRIDE * V:]).then_inc(x_in[par], 16)
                    pad = x[:, (T - 1) * V:].unsqueeze(1).broadcast_to([C, STRIDE, V])
                    sp.dma_start(xin[par][C:2 * C, (T - STRIDE) * V:].rearrange("c (t v) -> c t v", v=V),
                                 pad).then_inc(x_in[par], 16)

            sp.wait_ge(xT_stored, B * 16)
            sp.wait_ge(pad_stored, 16)
            with sp.Fori(0, B) as b:
                def load_rot(t):
                    sp.wait_ge(feat_ready, b * NT + t + 1)
                    sp.dma_start(rot[t % 2][:], a["c_rot"][t]).then_inc(rot_in[t % 2], 16)
                    sp.dma_start(xt[t % 2][:], xT_dram[:, bass.ds(b * S + t * P, P + 1)]).then_inc(xt_in[t % 2], 16)

                load_rot(0)
                load_rot(1)
                for t in range(NT):
                    if t + 2 < NT:
                        load_rot(t + 2)
                    sp.wait_ge(output_free, b * OUTPUTS + output_no["pk_out", t] + 2)
                    sp.dma_start(out[bass.ds(b, 1), t * P:(t + 1) * P, :].rearrange("b p d -> (b p) d"),
                                 outt[t % 2][:]).then_inc(out_done[t % 2], 16)
            for i in range(2):
                sp.wait_ge(out_done[i], 16 * (B * NT // 2) + 16)

        @block.gpsimd
        def _(pool):
            pool.wait_ge(consts_set, 1)
            pool.dma_start(xT_dram[:, B * S:B * S + 1], keys[0:D, 0, 200:201], allow_slow_non_contiguous=True).then_inc(pad_stored, 16)
            with pool.Fori(0, B) as b:
                pool.wait_ge(xT_kept, b + 1)
                pool.dma_start(xT_dram[:, bass.ds(b * S, S)], xTs).then_inc(xT_stored, 16)
                pool.wait_ge(xT_stored, b * 16 + 16)
                pool.sem_inc(xTs_free, 1)
            with pool.Fori(0, B) as b:
                for t in range(NT):
                    pool.wait_ge(index_ready, b * NT + t + 1)
                    for h in range(H2):
                        n = t * H2 + h
                        pool.wait_ge(rows_free, b * (NT * H2) + n + 1)
                        stand(pool)
                        for s in range(TOPK):
                            pool.indirect_dma_start(
                                rows[n % RING][:, s, :], None, a["kv"],
                                bass.IndirectOffsetOnAxis(index[t % 2][:, h * TOPK + s:h * TOPK + s + 1], 0),
                            ).then_inc(gathered[n % RING], 16)

        @block.tensor
        def _(pe):
            pe.wait_ge(weights_in, 16 * N_LOADS)
            for c in range(C * D // BANK):
                last = pe.matmul(ps[0:PATCH, c * BANK:(c + 1) * BANK], dft[:], w18[:, c * BANK:(c + 1) * BANK],
                                 start=True, stop=True)
            last.then_inc(w18_used, 1)
            pe.wait_ge(wtok_made, 1)
            pe.wait_ge(wtok_in, 32)
            with pe.Fori(0, B // 2) as i:
                for par in range(2):
                    b = i * 2 + par
                    pe.wait_ge(x_in[par], i * 48 + 48)
                    pe.wait_ge(k_kept, b + 1)
                    pe.wait_ge(tok_kept, b + 1)
                    xv = xin[par].rearrange("k (n p v) -> k p v n", p=STRIDE, v=V)
                    vs = BANK // NPATCH
                    for p in range(STRIDE):
                        for k in range(V // vs):
                            last = pe.matmul(ps[0:D, k * BANK:(k + 1) * BANK], wtok[:, p, :], xv[:, p, k * vs:(k + 1) * vs, :],
                                             start=(p == 0), stop=(p == STRIDE - 1))
                    last.then_inc(emb_made, 1)
                    pe.wait_ge(emb_kept, b + 1)
                    stand(pe)
                    for k in range(NTOK):
                        last = pe.transpose(ps[:, k * D:(k + 1) * D], embT[:, k * P:(k + 1) * P], ident[0:D, 0:D])
                    last.then_inc(tok_made, 1)
                    pe.wait_ge(v_kept, b + 1)
                    pe.wait_ge(ln_made, b + 1)
                    stand(pe)
                    for k in range(NT):
                        last = pe.transpose(ps[0:D, (2 + k // 4) * BANK + (k % 4) * P:(2 + k // 4) * BANK + (k % 4 + 1) * P],
                                            ln_n[:, k, :], ident[:])
                    last.then_inc(xT_made, 1)
                    pe.wait_ge(xT_kept, b + 1)
                    for c in range(3):
                        last = pe.matmul(ps[:, (5 + c) * BANK:(6 + c) * BANK], wk2[:], xTs[:, c * BANK:(c + 1) * BANK],
                                         start=True, stop=True)
                    last.then_inc(k_made, 1)
                    for k in range(NT):
                        last = pe.matmul(ps[:, 2 * BANK + k * D:2 * BANK + (k + 1) * D], xTs[:, k * P:(k + 1) * P], wv[:],
                                         start=True, stop=True)
                    last.then_inc(v_made, 1)
            pe.wait_ge(k_kept, B + 1)
            pe.wait_ge(v_kept, B + 1)

            with pe.Fori(0, B) as b:
                def misc_slot(key, ahead=0):
                    pe.wait_ge(misc_kept, b * MISCS + misc_no[key] + 1 + ahead)

                def score_slot(key):
                    pe.wait_ge(scores_free, b * SCORES + score_no[key] + 1)

                def output_slot(key, ahead=0):
                    pe.wait_ge(output_free, b * OUTPUTS + output_no[key] + 1 + ahead)

                def queries(t):
                    misc_slot(("q", t))
                    pe.wait_ge(xt_in[t % 2], b * (NT // 2) * 16 + 16 * (t // 2) + 16)
                    pe.matmul(M_ps[:, 0:P + 1], wq2[:], xt[t % 2][:],
                              start=True, stop=True).then_inc(misc_ready, 1)
                    misc_slot(("q", t), 1)
                    score_slot(("rot", t))
                    stand(pe)
                    for kind in range(2):
                        for v in range(2):
                            for h in range(H1):
                                c = (kind * 2 + v) * BANK + h * P
                                last = pe.matmul(S_ps[0:D, c:c + P], wpos[:, v, h, :], qq[0:D, kind:kind + P],
                                                 start=True, stop=True)
                    last.then_inc(scores_ready, 1)

                def rel_scores(t, h):
                    if h == 0:
                        pe.wait_ge(feat_ready, b * NT + t + 3)
                    score_slot(("rel", t, h))
                    seam_at = (t + 1) * P
                    for kind, lo, hi in ((0, 0, seam_at), (1, seam_at, S)):
                        c = lo
                        while c < hi:
                            e = min(hi, (c // BANK + 1) * BANK)
                            q = (kind * H1 + h) * P
                            pe.matmul(S_ps[:, c:e], qfeat[:, q:q + P], kfeat[:, bass.ds(b * S + c, e - c)],
                                      start=True, stop=True)
                            c = e
                    q = (H1 + h) * P
                    pe.matmul(X_ps[:, 0:P], qfeat[:, q:q + P], kfeat[:, bass.ds(b * S + t * P, P)],
                              start=True, stop=True)
                    q = (2 * H1 + h) * P
                    w = P + 1 if t + 1 < NT else P
                    pe.matmul(X_ps[:, P:P + w], qfeat[:, q:q + P], kfeat[:, bass.ds(b * S + t * P, w)],
                              start=True, stop=True).then_inc(scores_ready, 1)

                def pk_scores(t, h):
                    score_slot(("pk", t, h))
                    p0 = (h % 2) * DH2
                    n = (t + 1) * P
                    for c in range(0, n, BANK):
                        e = min(n, c + BANK)
                        last = pe.matmul(S_ps[:, c:e], q2T[t % 2][p0:p0 + DH2, h // 2, :], kT[p0:p0 + DH2, h // 2, c:e],
                                         start=True, stop=True)
                    last.then_inc(scores_ready, 1)

                def turn(key, tiles):
                    pe.wait_ge(scores_free, b * SCORES + score_no[key] + 2)
                    par = unit_no[key] % 2
                    for g in range(-(-tiles // 4)):
                        n = group_no[key] + g
                        pe.wait_ge(turned_kept, b * GROUPS + n + 1)
                        for j in range(4 * g, min(tiles, 4 * g + 4)):
                            last = pe.transpose(T_ps[n % 2][:, (j % 4) * P:(j % 4 + 1) * P],
                                                probs[par][:, j * P:(j + 1) * P], ident[:])
                        last.then_inc(turned, 1)

                def weigh(key, tiles):
                    kind, t, h = key
                    par = unit_no[key] % 2
                    pe.wait_ge(turned_kept, b * GROUPS + group_no[key] + -(-tiles // 4) + 2)
                    output_slot(key)
                    for j in range(tiles):
                        if kind == "rel":
                            o = O_ps[:, h * DH1:(h + 1) * DH1]
                            val = v1[:, bass.ds(b * NT + j, 1), h * DH1:(h + 1) * DH1].rearrange("p a d -> p (a d)")
                        else:
                            o = O_ps[:, D + par * DH2:D + (par + 1) * DH2]
                            val = v2[:, j, h, :]
                        last = pe.matmul(o, probsT[par][:, j * P:(j + 1) * P], val, start=(j == 0), stop=(j == tiles - 1))
                    last.then_inc(pv_ready, 1)

                def units(keys_, tiles, first):
                    first(keys_[0][1], keys_[0][2])
                    for n, key in enumerate(keys_):
                        turn(key, tiles)
                        if n + 1 < len(keys_):
                            first(keys_[n + 1][1], keys_[n + 1][2])
                        weigh(key, tiles)

                def relative(t):
                    queries(t)
                    units([("rel", t, h) for h in range(H1)], NT, rel_scores)
                    output_slot(("rel", t, H1 - 1), 1)
                    misc_slot(("ctxT", t))
                    stand(pe)
                    pe.transpose(M_ps[0:D, 0:P], ctx1[:], ident[:]).then_inc(misc_ready, 1)
                    misc_slot(("ctxT", t), 1)
                    output_slot(("rel_out", t))
                    stand(pe)
                    pe.matmul(REL_OUT, ctxT[:], wout[:], start=True, stop=True).then_inc(rel_out, 1)
                    pe.wait_ge(x2_ready, b * NT + t + 1)
                    misc_slot(("xT", t))
                    stand(pe)
                    pe.transpose(M_ps[0:D, 0:P], tl_n[:, 0, :], ident[:]).then_inc(misc_ready, 1)
                    misc_slot(("xT", t), 1)
                    for q in range(4):
                        last = pe.matmul(M_ps[:, q * P:(q + 1) * P], wqf[:, q * P:(q + 1) * P], x2T[:], start=True, stop=True)
                    last.then_inc(misc_ready, 1)
                    misc_slot(("qT", t), 1)
                    for q in range(4):
                        last = pe.matmul(M_ps[:, q * P:(q + 1) * P], wpk[:, q * P:(q + 1) * P], x2T[:], start=True, stop=True)
                    last.then_inc(misc_ready, 1)
                    misc_slot(("pkT", t), 1)
                    score_slot(("sim", t))
                    for q in range(4):
                        last = pe.matmul(S_ps[:, q * 4 * NKEY:(q + 1) * 4 * NKEY], pkT[:, q, :], keys[:, q, :],
                                         start=True, stop=True)
                    last.then_inc(scores_ready, 1)

                def product_key(t):
                    for pair in range(H2 // 2):
                        pe.wait_ge(k2_ready, b * (NT * 4) + t * 4 + pair + 1)
                        misc_slot(("kT", t, pair))
                        pe.transpose(M_ps[:, 0:P], k2[:, pair, :], ident[:]).then_inc(misc_ready, 1)
                        misc_slot(("kT", t, pair), 1)
                        units([("pk", t, 2 * pair), ("pk", t, 2 * pair + 1)], t + 1, pk_scores)
                    output_slot(("pk", t, H2 - 1), 1)
                    misc_slot(("oT", t))
                    for q in range(4):
                        last = pe.transpose(M_ps[:, q * P:(q + 1) * P], ao[:, q * P:(q + 1) * P], ident[:])
                    last.then_inc(misc_ready, 1)
                    misc_slot(("oT", t), 1)
                    output_slot(("pk_out", t))
                    for q in range(4):
                        last = pe.matmul(PK_OUT, aoT[:, q, :], wo[:, q, :], start=(q == 0), stop=(q == 3))
                    last.then_inc(pk_out, 1)

                relative(0)
                for t in range(NT):
                    if t + 1 < NT:
                        relative(t + 1)
                    product_key(t)

        @block.scalar
        def _(act):
            act.sem_inc(scores_free, 1)
            act.sem_inc(turned_kept, 2)
            act.sem_inc(misc_kept, 1)
            act.sem_inc(tok_kept, 1)
            act.sem_inc(k_kept, 1)
            act.sem_inc(tok_made, 2)
            act.sem_inc(v_made, 1)
            act.sem_inc(xT_made, 1)
            act.sem_inc(xTs_free, 1)
            act.wait_ge(w18_used, 1)
            act.activation(wtok_p[:, 0:2048], ps[0:PATCH, 0:2048], ACT.Copy)
            act.activation(wtok_p[:, 2048:4096], ps[0:PATCH, 2048:4096], ACT.Copy).then_inc(wtok_made, 1)
            with act.Fori(0, B) as b:
                act.wait_ge(emb_made, b + 1)
                act.activation(embT, ps[0:D, 0:NTOK * P], ACT.Copy).then_inc(emb_kept, 1)
                act.wait_ge(tok_made, b + 3)
                act.activation(h0[:, bass.ds(b * NT, NTOK), :].rearrange("p t d -> p (t d)"), ps[:, 0:NTOK * D],
                               ACT.Copy).then_inc(tok_kept, 1)
                for k in range(2):
                    act.wait_ge(var_ready, b * 2 + k + 1)
                    act.activation(stat[:, 3, :], stat[:, 2, :], ACT.Sqrt).then_inc(dev_ready, 1)
                act.wait_ge(xT_made, b + 2)
                act.wait_ge(v_made, b + 1)
                act.wait_ge(xTs_free, b + 1)
                act.activation(xTs, ps[0:D, 2 * BANK:5 * BANK], ACT.Copy).then_inc(xT_kept, 1)
                act.wait_ge(k_made, b + 1)
                act.activation(kfeat[D:P, bass.ds(b * S, S)], ps[D:P, 5 * BANK:8 * BANK], ACT.Identity,
                               bias=bk2[D:P, 0:1]).then_inc(k_kept, 1)

            with act.Fori(0, B) as b:
                def copy_misc(key, dst, src, func=ACT.Copy, **kw):
                    act.wait_ge(misc_ready, b * MISCS + misc_no[key] + 1)
                    act.activation(dst, src, func, **kw).then_inc(misc_kept, 1)

                def exps(key, tiles):
                    par = unit_no[key] % 2
                    act.wait_ge(max_ready, b * UNITS + unit_no[key] + 1)
                    act.activation(probs[par][:, 0:tiles * P], S_ps[:, 0:tiles * P], ACT.Exp,
                                   bias=rowmax[:, par:par + 1], accum_out=rowsum[:, par:par + 1]).then_inc(scores_free, 1)

                def copy_turned(key, tiles):
                    par = unit_no[key] % 2
                    act.wait_ge(pv_ready, b * UNITS + unit_no[key] + 1)
                    for g in range(-(-tiles // 4)):
                        n = group_no[key] + g
                        act.wait_ge(turned, b * GROUPS + n + 1)
                        w = min(tiles - 4 * g, 4) * P
                        act.activation(probsT[par][:, g * BANK:g * BANK + w], T_ps[n % 2][:, 0:w],
                                       ACT.Copy).then_inc(turned_kept, 1)

                def units(keys_, tiles):
                    exps(keys_[0], tiles)
                    for n, key in enumerate(keys_):
                        copy_turned(key, tiles)
                        if n + 1 < len(keys_):
                            exps(keys_[n + 1], tiles)

                def relative(t):
                    copy_misc(("q", t), qq[:], M_ps[:, 0:P + 1], ACT.Identity, bias=bquv[:, 0:1])
                    units([("rel", t, h) for h in range(H1)], NT)
                    copy_misc(("ctxT", t), ctxT[:], M_ps[0:D, 0:P])
                    act.wait_ge(var_ready, b * NT + t + 1 + 2 * B)
                    act.activation(stat[:, 3, 0:1], stat[:, 2, 0:1], ACT.Sqrt).then_inc(dev_ready, 1)
                    copy_misc(("xT", t), x2T[:], M_ps[0:D, 0:P])
                    copy_misc(("qT", t), q2T[t % 2][:].rearrange("p a b -> p (a b)"), M_ps, ACT.Copy, scale=DH2 ** -0.5)
                    copy_misc(("pkT", t), pkT.rearrange("p a b -> p (a b)"), M_ps)
                    act.wait_ge(scores_ready, b * SCORES + score_no["sim", t] + 1)
                    act.activation(sim.rearrange("p l k -> p (l k)"), S_ps[:, 0:1024], ACT.Copy).then_inc(scores_free, 1)
                    act.wait_ge(exp_asked, b * NT + t + 1)
                    act.activation(fin[:], fin[:], ACT.Exp).then_inc(exp_made, 1)

                relative(0)
                for t in range(NT):
                    if t + 1 < NT:
                        relative(t + 1)
                    for pair in range(H2 // 2):
                        copy_misc(("kT", t, pair), kT[:, pair, t * P:(t + 1) * P], M_ps[:, 0:P])
                        units([("pk", t, 2 * pair), ("pk", t, 2 * pair + 1)], t + 1)
                    copy_misc(("oT", t), aoT[:].rearrange("p a b -> p (a b)"), M_ps)

        @block.vector
        def _(dve):
            def layer_norm(src, dst, sq, n, asked):
                mean, ssum, var, dev, inv, tmp = (stat[:, k, 0:n] for k in range(6))
                dve.tensor_reduce(ssum, src, AX.X, ALU.add)
                dve.drain()
                dve.tensor_scalar(mean, ssum, 1.0 / D, None, ALU.mult)
                dve.drain()
                dve.tensor_tensor(dst, src, mean.unsqueeze(2).broadcast_to([P, n, D]), ALU.subtract)
                dve.drain()
                dve.tensor_tensor(sq, dst, dst, ALU.mult)
                dve.drain()
                dve.tensor_reduce(ssum, sq, AX.X, ALU.add)
                dve.drain()
                dve.tensor_scalar(var, ssum, 1.0 / D, EPS, ALU.mult, ALU.add).then_inc(var_ready, 1)
                dve.wait_ge(dev_ready, asked)
                dve.reciprocal(inv, dev)
                dve.drain()
                dve.tensor_tensor(tmp, inv, inv, ALU.mult)
                dve.drain()
                dve.tensor_tensor(tmp, tmp, var, ALU.mult)
                dve.drain()
                dve.tensor_scalar(tmp, tmp, -0.5, 1.5, ALU.mult, ALU.add)
                dve.drain()
                dve.tensor_tensor(inv, inv, tmp, ALU.mult)
                dve.drain()
                dve.tensor_tensor(dst, dst, inv.unsqueeze(2).broadcast_to([P, n, D]), ALU.mult)
                dve.drain()

            dve.memset(keys[:], 0.0).then_inc(consts_set, 1)
            dve.sem_inc(v_kept, 1)
            dve.sem_inc(feat_ready, 2)
            dve.sem_inc(pv_ready, 2)
            dve.sem_inc(output_free, 1)
            dve.sem_inc(rows_free, RING)
            dve.wait_ge(weights_in, 16 * N_LOADS)
            dve.tensor_tensor(bquv[:], bq2[:], uv2[:], ALU.add).then_inc(bias_made, 1)
            with dve.Fori(0, B) as b:
                dve.wait_ge(tok_kept, b + 2)
                dve.wait_ge(xT_made, b + 1)
                layer_norm(h0[:, bass.ds(b * NT, NT), :], ln_n, ln_q, NT, b * 2 + 1)
                layer_norm(ln_n, ln_n, ln_q, NT, b * 2 + 2)
                dve.tensor_tensor(ln_n, ln_n, gamma[:].unsqueeze(1).broadcast_to([P, NT, D]), ALU.mult)
                dve.drain()
                dve.tensor_tensor(ln_n, ln_n, beta[:].unsqueeze(1).broadcast_to([P, NT, D]), ALU.add).then_inc(ln_made, 1)
                dve.wait_ge(v_made, b + 2)
                dve.tensor_tensor(v1[:, bass.ds(b * NT, NT), :],
                                  ps[:, 2 * BANK:2 * BANK + NT * D].rearrange("p (t d) -> p t d", t=NT),
                                  bv[:].unsqueeze(1).broadcast_to([P, NT, D]), ALU.add).then_inc(v_kept, 1)

            dve.memset(qfeat[0:D, 2 * H1 * P:3 * H1 * P], 0.0)
            with dve.Fori(0, B) as b:
                def features(t):
                    dve.wait_ge(misc_kept, b * MISCS + misc_no["q", t] + 2)
                    dve.wait_ge(scores_ready, b * SCORES + score_no["rot", t] + 1)
                    dve.wait_ge(rot_in[t % 2], b * (NT // 2) * 16 + 16 * (t // 2) + 16)
                    dve.tensor_tensor(rot_prod.rearrange("p (k h i) -> p k h i", k=4, h=H1),
                                      S_ps[0:D, :].rearrange("p (k h i) -> p k h i", k=4, h=H1),
                                      rot[t % 2][:].unsqueeze(2).broadcast_to([D, 4, H1, P]),
                                      ALU.mult).then_inc(scores_free, 1)
                    dve.tensor_tensor(qfeat[D:P, :].rearrange("p (k i) -> p k i", i=P),
                                      qq[D:P, 0:P].unsqueeze(1).broadcast_to([D, 3 * H1, P]),
                                      own[D:P, :].unsqueeze(2).broadcast_to([D, 3 * H1, P]), ALU.mult)
                    dve.drain()
                    r = rot_prod.rearrange("p (k v n) -> p k v n", k=2, v=2)
                    dve.tensor_tensor(qfeat[0:D, 0:2 * H1 * P].rearrange("p (k n) -> p k n", k=2),
                                      r[:, :, 0, :], r[:, :, 1, :], ALU.add).then_inc(feat_ready, 1)

                def rel_max(t, h):
                    key = ("rel", t, h)
                    par = unit_no[key] % 2
                    dve.wait_ge(scores_ready, b * SCORES + score_no[key] + 1)
                    stand(dve)
                    dve.copy_predicated(S_ps[:, t * P:(t + 1) * P], upper[:], X_ps[:, 0:P])
                    dve.drain()
                    w = P + 1 if t + 1 < NT else P
                    dve.copy_predicated(S_ps[:, t * P:t * P + w], seam[:, 0:w], X_ps[:, P:P + w])
                    dve.drain()
                    dve.tensor_reduce(rowmax[:, par:par + 1], S_ps[:, 0:S], AX.X, ALU.max, negate=True).then_inc(max_ready, 1)

                def pk_max(t, h):
                    key = ("pk", t, h)
                    par = unit_no[key] % 2
                    dve.wait_ge(scores_ready, b * SCORES + score_no[key] + 1)
                    dve.tensor_tensor(S_ps[:, t * P:(t + 1) * P], S_ps[:, t * P:(t + 1) * P], future[:], ALU.add)
                    dve.drain()
                    dve.tensor_reduce(rowmax[:, par:par + 1], S_ps[:, 0:(t + 1) * P], AX.X, ALU.max,
                                      negate=True).then_inc(max_ready, 1)

                def normalise(key):
                    kind, t, h = key
                    par = unit_no[key] % 2
                    dve.wait_ge(pv_ready, b * UNITS + unit_no[key] + 3)
                    dve.reciprocal(rowinv[:, par:par + 1], rowsum[:, par:par + 1])
                    dve.drain()
                    if kind == "rel":
                        ins = dve.tensor_scalar(ctx1[:, h * DH1:(h + 1) * DH1], O_ps[:, h * DH1:(h + 1) * DH1],
                                                rowinv[:, par:par + 1], None, ALU.mult)
                    else:
                        ins = dve.tensor_scalar(ao[:, h * DH2:(h + 1) * DH2], O_ps[:, D + par * DH2:D + (par + 1) * DH2],
                                                rowinv[:, par:par + 1], None, ALU.mult)
                    ins.then_inc(output_free, 1)

                def mix_rows(t, h):
                    n = t * H2 + h
                    g = rows[n % RING]
                    dve.wait_ge(gathered[n % RING], b * (NT * H2 // RING * TOPK * 16) + (n // RING + 1) * TOPK * 16)
                    dve.tensor_tensor(g, g, weight[t % 2][:, h, :].unsqueeze(2).broadcast_to([P, TOPK, 2 * DH2]), ALU.mult)
                    dve.drain()
                    gd = g.rearrange("p s d -> p d s")
                    dve.tensor_reduce(k2[:, h // 2, (h % 2) * DH2:(h % 2 + 1) * DH2], gd[:, 0:DH2, :], AX.X, ALU.add)
                    ins = dve.tensor_reduce(v2[:, t, h, :], gd[:, DH2:2 * DH2, :], AX.X, ALU.add).then_inc(rows_free, 1)
                    if h % 2:
                        dve.drain().then_inc(k2_ready, 1)

                def after_attention(t):
                    dve.wait_ge(rel_out, b * NT + t + 1)
                    dve.tensor_tensor(tl_q[:, 0, :], REL_OUT, bout[:], ALU.add).then_inc(output_free, 1)
                    dve.drain()
                    dve.tensor_tensor(h1[t % 2][:], tl_q[:, 0, :],
                                      h0[:, bass.ds(b * NT + t, 1), :].rearrange("p a d -> p (a d)"), ALU.add)
                    dve.drain()
                    layer_norm(h1[t % 2][:].unsqueeze(1), tl_n[:], tl_q[:], 1, b * NT + t + 1 + 2 * B)
                    dve.drain().then_inc(x2_ready, 1)

                def select(t):
                    dve.wait_ge(scores_free, b * SCORES + score_no["sim", t] + 2)
                    stand(dve)
                    for l in range(16):
                        dve.max(best[:, l, 0:8], sim[:, l, :])
                    dve.drain()
                    for l in range(16):
                        dve.match_replace(sim_rest[:, l, :], best[:, l, 0:8], sim[:, l, :], LOWEST)
                        dve.max_index(best_i[:, l, 0:8], best[:, l, 0:8], sim[:, l, :])
                    dve.drain()
                    for l in range(16):
                        dve.max(best[:, l, 8:16], sim_rest[:, l, :])
                    dve.drain()
                    for l in range(16):
                        dve.max_index(best_i[:, l, 8:16], best[:, l, 8:16], sim_rest[:, l, :])
                    dve.drain()
                    dve.scalar_tensor_tensor(out=i1s[:].rearrange("p h r -> p (h r)"),
                                             in0=best_i[:, H2:2 * H2, :].rearrange("p h r -> p (h r)"), scalar=float(NKEY),
                                             in1=offs[:], op0=ALU.mult, op1=ALU.add)
                    dve.drain()
                    for c, first, second in ((cand, best[:, 0:H2, :], best[:, H2:2 * H2, :]), (cand_i, best_i[:, 0:H2, :], i1s[:])):
                        at = 0
                        for r0, n in SPANS:
                            if n == 1:
                                break
                            dve.tensor_tensor(c[:, :, at:at + n], second[:, :, 0:n],
                                              first[:, :, r0:r0 + 1].broadcast_to([P, H2, n]), ALU.add)
                            at += n
                        dve.tensor_tensor(c[:, :, at:NCAND], first[:, :, r0:TOPK],
                                          second[:, :, 0:1].broadcast_to([P, H2, TOPK - r0]), ALU.add)
                    dve.drain()
                    for h in range(H2):
                        dve.max(fin[:, h, 0:8], cand[:, h, :])
                    dve.drain()
                    for h in range(H2):
                        dve.match_replace(cand_rest[:, h, :], fin[:, h, 0:8], cand[:, h, :], LOWEST)
                        dve.max_index(fin_pos[:, h, 0:8], fin[:, h, 0:8], cand[:, h, :])
                    dve.drain()
                    for h in range(H2):
                        dve.max(fin[:, h, 8:16], cand_rest[:, h, :])
                    dve.drain()
                    for h in range(H2):
                        dve.max_index(fin_pos[:, h, 8:16], fin[:, h, 8:16], cand_rest[:, h, :])
                    dve.drain()
                    dve.tensor_copy(fsum[:], fin[:, :, 0])
                    dve.drain()
                    dve.tensor_tensor(fin[:], fin[:], fsum[:].unsqueeze(2).broadcast_to([P, H2, TOPK]),
                                      ALU.subtract).then_inc(exp_asked, 1)
                    for half in range(2):
                        hs = slice(4 * half, 4 * half + 4)
                        m = match.rearrange("p (j c) -> p j c", c=NCAND)
                        dve.tensor_tensor(m, iota[:].unsqueeze(1).broadcast_to([P, 4 * TOPK, NCAND]),
                                          fin_pos[:, hs, :].rearrange("p h k -> p (h k)").unsqueeze(2)
                                          .broadcast_to([P, 4 * TOPK, NCAND]), ALU.is_equal)
                        dve.drain()
                        m4 = match.rearrange("p (h k c) -> p h k c", h=4, k=TOPK)
                        dve.tensor_tensor(m4, m4, cand_i[:, hs, :].unsqueeze(2).broadcast_to([P, 4, TOPK, NCAND]), ALU.mult)
                        dve.drain()
                        dve.tensor_reduce(picked[:], m, AX.X, ALU.add)
                        dve.drain()
                        ins = dve.tensor_copy(index[t % 2][:, half * 4 * TOPK:(half + 1) * 4 * TOPK], picked[:])
                        if half:
                            ins.then_inc(index_ready, 1)
                        else:
                            dve.drain()
                    dve.wait_ge(exp_made, b * NT + t + 1)
                    dve.tensor_reduce(fsum[:], fin[:], AX.X, ALU.add)
                    dve.drain()
                    dve.reciprocal(fsum[:], fsum[:])
                    dve.drain()
                    dve.tensor_tensor(weight[t % 2][:], fin[:], fsum[:].unsqueeze(2).broadcast_to([P, H2, TOPK]), ALU.mult)
                    dve.drain()

                def relative(t, between):
                    features(t)
                    rel_max(t, 0)
                    for h in range(H1):
                        if h in between:
                            mix_rows(*between[h])
                        if h + 1 < H1:
                            rel_max(t, h + 1)
                        normalise(("rel", t, h))
                    after_attention(t)
                    select(t)

                def product_key(t, pair):
                    pk_max(t, 2 * pair)
                    pk_max(t, 2 * pair + 1)
                    normalise(("pk", t, 2 * pair))
                    normalise(("pk", t, 2 * pair + 1))

                relative(0, {})
                for t in range(NT):
                    if t + 1 < NT:
                        relative(t + 1, {0: (t, 0), 2: (t, 1)})
                    else:
                        mix_rows(t, 0)
                        mix_rows(t, 1)
                    mix_rows(t, 2)
                    mix_rows(t, 3)
                    product_key(t, 0)
                    mix_rows(t, 4)
                    product_key(t, 1)
                    mix_rows(t, 5)
                    product_key(t, 2)
                    mix_rows(t, 6)
                    mix_rows(t, 7)
                    product_key(t, 3)
                    dve.wait_ge(pk_out, b * NT + t + 1)
                    dve.wait_ge(out_done[t % 2], b * (NT // 2) * 16 + 16 * (t // 2) + 16)
                    dve.tensor_tensor(outt[t % 2][:], PK_OUT, h1[t % 2][:], ALU.add).then_inc(output_free, 1)


def kernel(**inputs):
    import concourse.bacc as bacc
    from concourse.bass_utils import run_bass_kernel_spmd

    i = {k: np.asarray(v) for k, v in inputs.items()}
    wpos = i["L0_attn_Wpos"]
    turned = wpos.T.reshape(H1, DH1, D)
    folded = np.zeros((D, 2, H1, D), np.float32)
    for h in range(H1):
        folded[h * DH1:(h + 1) * DH1, 0, h] = np.concatenate([turned[h][:, 0::2], turned[h][:, 1::2]], 1)
        folded[h * DH1:(h + 1) * DH1, 1, h] = np.concatenate([turned[h][:, 1::2], turned[h][:, 0::2]], 1)
    bq, u, v = i["L0_attn_bq"], i["L0_attn_u_bias"].reshape(-1), i["L0_attn_v_bias"].reshape(-1)
    bk = i["L0_attn_bk"]
    arrays = {
        "x": i["x"], "txt": i["txt"],
        "w18": i["L0_tok_W"].reshape(D, 2 * FREQ, C).transpose(1, 2, 0).reshape(2 * FREQ, C * D),
        "wq2": np.concatenate([i["L0_attn_Wq"]] * 2, 1), "wk2": np.concatenate([i["L0_attn_Wk"]] * 2, 1),
        "wv": i["L0_attn_Wv"], "wout": i["L0_attn_Wout"], "wpos": folded,
        "bq2": np.concatenate([bq, bq])[:, None], "uv2": np.concatenate([v, u])[:, None],
        "bk2": np.concatenate([bk, bk])[:, None],
        "bv": i["L0_attn_bv"], "bout": i["L0_attn_bout"], "gamma": i["L0_attn_ln_gamma"], "beta": i["L0_attn_ln_beta"],
        "wqf": i["L0_ffn_Wq"], "wpk": i["L0_ffn_Wq_pk"], "wo": i["L0_ffn_Wo"],
        "keys": i["L0_ffn_pk_keys"].transpose(0, 2, 3, 1).reshape(4, 4, DKEY, NKEY),
        "kv": np.concatenate([i["L0_ffn_keys_table"], i["L0_ffn_values_table"]], 1),
        **shape_constants(),
    }
    arrays = {k: np.ascontiguousarray(v) for k, v in arrays.items()}
    nc = bacc.Bacc("TRN2", target_bir_lowering=False, num_devices=1)
    nc.disable_value_cache = True
    aps = {k: nc.dram_tensor(f"in_{k}", v.shape, mybir.dt.from_np(v.dtype), kind="ExternalInput").ap()
           for k, v in arrays.items()}
    out = nc.dram_tensor("out_0", (B, S, D), F32, kind="ExternalOutput").ap()
    program(nc, aps, out)
    r = run_bass_kernel_spmd(nc, [{f"in_{k}": v for k, v in arrays.items()}], core_ids=[0])
    return r.results[0]["out_0"]
```

```python
from contextlib import ExitStack

import numpy as np

import concourse.bass as bass
from concourse import mybir

F32 = mybir.dt.float32
U32 = mybir.dt.uint32
I32 = mybir.dt.int32
ALU = mybir.AluOpType
ACT = mybir.ActivationFunctionType
AX = mybir.AxisListType

P = 128
B, C, T, V = 4, 64, 128, 64
PATCH, STRIDE = 16, 8
NPATCH = (T + STRIDE - PATCH) // STRIDE + 1
FREQ = PATCH // 2 + 1
D = 64
TXT = 512
S = V * NPATCH + TXT
NT = S // P
NTOK = V * NPATCH // P
H1, DH1 = 4, 16
H2, DH2 = 8, 64
NKEY, TOPK, DKEY = 64, 16, 32
NKV = NKEY * NKEY
EPS = 1e-5
LOWEST = -3.0e38
BANK = 512

SPANS = [(r0, TOPK // (r0 + 1)) for r0 in range(TOPK)]
NCAND = sum(n for _, n in SPANS)
RING = 4


def shape_constants():
    div = np.exp(np.arange(0, D, 2, dtype=np.float32) * np.float32(-np.log(10000.0) / D)).astype(np.float64)
    pos = np.arange(S, dtype=np.float64)
    ang = div[:, None] * pos[None, :]
    pe = np.concatenate([np.sin(ang), np.cos(ang)], 0).astype(np.float32)
    lo = div[:, None] * (S - 1 - pos)[None, :]
    up = div[:, None] * (-(pos + 2))[None, :]
    root = np.sqrt(float(D))
    rot = np.stack([np.concatenate([f, g], 0) / root for a in (lo, up)
                    for f, g in ((np.cos(a), np.cos(a)), (-np.sin(a), np.sin(a)))], 1).astype(np.float32)
    rot = np.ascontiguousarray(rot.reshape(D, 4, NT, P).transpose(2, 0, 1, 3))
    i, j = np.arange(P)[:, None], np.arange(P + 1)[None, :]
    upper = (j[:, :P] >= i + 2).astype(np.int32)
    seam = (j == i + 1).astype(np.int32)
    future = np.where(j[:, :P] > i, np.float32(LOWEST), np.float32(0)).astype(np.float32)
    own = np.zeros((P, 3, H1), np.float32)
    for h in range(H1):
        own[D + h * DH1:D + (h + 1) * DH1, :, h] = 1.0 / root
    iota = np.tile(np.arange(NCAND, dtype=np.float32), (P, 1))
    offs = np.tile(np.repeat(np.arange(H2, dtype=np.float32) * NKV, TOPK), (P, 1))
    p, f = np.arange(PATCH)[None, :], np.arange(FREQ)[:, None]
    t = 2 * np.pi * f * p / PATCH
    dft = (np.concatenate([np.cos(t), -np.sin(t)], 0) / np.sqrt(float(PATCH))).astype(np.float32)
    return {"c_pe": pe, "c_rot": rot, "c_upper": upper, "c_seam": seam, "c_future": future,
            "c_own": own.reshape(P, 3 * H1), "c_iota": iota, "c_offs": offs, "c_dft": dft,
            "c_ident": np.eye(P, dtype=np.float32)}


SELECT_PARTS = 8


def steps(after=True):
    def select(t, *parts):
        return [("select", t, n) for n in parts]

    order = []
    for t in range(NT):
        if t == 0:
            row = [("rel", 2, 0), ("mix", 0, 2), ("rel", 2, 1), ("mix", 0, 3), ("kT", 0, 0), ("rel", 2, 2), ("mix", 0, 4),
                   ("rel", 2, 3), ("kT", 0, 1), ("project", 2), ("ln", 2), ("mix", 0, 5), ("norm", 2), ("q", 3), ("sim", 2),
                   ("mix", 0, 6), ("kT", 0, 2), ("rot", 3)]
        else:
            early = [] if t == 1 else [("mix", t - 1, 3)]
            row = ([("rel", t + 2, 0), ("store", t - 2)] + early +
                   [("pk", t - 1, 0)] + (select(t, 7) if t > 1 else []) +
                   [("rel", t + 2, 1)] + ([("kT", t - 1, 1), ("mix", t - 1, 4)] if t > 1 else []) +
                   [("pk", t - 1, 1)] + select(t + 1, 0) +
                   [("rel", t + 2, 2), ("mix", t - 1, 5 if t > 1 else 7), ("pk", t - 1, 2)] + select(t + 1, 1, 2) +
                   [("rel", t + 2, 3)] + ([("kT", t - 1, 2), ("mix", t - 1, 6)] if t > 1 else []) + [("project", t + 2)] +
                   [("pk", t - 1, 3)] + ([("mix", t - 1, 7)] if t > 1 else []) + [
                    ("pk", t - 1, 4), ("ln", t + 2), ("kT", t - 1, 3), ("pk", t - 1, 5), ("mix", t, 0)] + select(t + 1, 3) +
                   [("norm", t + 2), ("q", t + 3), ("pk", t - 1, 6), ("sim", t + 2)] + select(t + 1, 4, 5, 6) +
                   [("pk", t - 1, 7), ("mix", t, 1), ("rot", t + 3), ("final", t - 1), ("mix", t, 2), ("kT", t, 0)])
        limit = NT + 3 if after else NT
        order += [s for s in row if 0 <= s[1] < limit]
    t = NT - 1
    e = [("pk", t, h) for h in range(H2)]
    s = select(NT + 1, *range(SELECT_PARTS))
    tail = ([e[0], ("store", t - 1), ("mix", t, 3), ("kT", t, 1)] + select(NT, 7) +
            [e[1], ("mix", t, 4), e[2], ("mix", t, 5), ("kT", t, 2), e[3], ("mix", t, 6), e[4], ("mix", t, 7), s[0],
             e[5], ("kT", t, 3), s[1], e[6], s[2], ("mix", NT, 0), e[7], s[3], s[4], ("final", t), s[5],
             ("store", t), ("mix", NT, 1), s[6], s[7]])
    return order + [s for s in tail if after or s[1] < NT]


def opening():
    order = [("q", 0), ("rot", 0)] + [("rel", 0, h) for h in range(H1)]
    order += [("project", 0), ("ln", 0), ("norm", 0), ("q", 1), ("sim", 0)]
    s = [("select", 0, n) for n in range(SELECT_PARTS)]
    order += s[0:1] + [("rot", 1)] + s[1:4]
    for h in range(H1):
        order += [("rel", 1, h), s[4 + h]]
    order += [("project", 1), ("mix", 0, 0), ("ln", 1), ("norm", 1), ("q", 2), ("sim", 1), ("mix", 0, 1)]
    s = [("select", 1, n) for n in range(SELECT_PARTS)]
    return order + s[0:1] + [("rot", 2)] + s[1:]


def tiles_of(step):
    return NT if step[0] == "rel" else step[1] + 1


def numbered(order):
    uses = {"scores": {}, "unit": {}, "turned": {}, "misc": {}, "output": {}}
    total = dict.fromkeys(uses, 0)

    def take(what, key, n=1):
        uses[what][key] = total[what]
        total[what] += n

    for step in order:
        kind, t = step[:2]
        if kind in ("rel", "pk"):
            for what in ("scores", "unit", "output"):
                take(what, step)
            take("turned", step, -(-tiles_of(step) // 4))
        elif kind in ("rot", "sim"):
            take("scores", step)
        elif kind in ("q", "kT"):
            take("misc", step)
        elif kind == "project":
            take("misc", ("ctxT", t))
            take("output", step)
        elif kind == "norm":
            for name in ("xT", "qT", "pkT"):
                take("misc", (name, t))
        elif kind == "final":
            take("misc", ("oT", t))
            take("output", step)
    return uses, total


def next_scores(order, n):
    for i in range(n + 1, len(order)):
        kind, t = order[i][:2]
        if kind in ("rel", "pk", "rot", "sim"):
            source = {"rot": ("q", t), "sim": ("norm", t), "pk": ("kT", t, order[i][-1] // 2)}.get(kind)
            return order[i] if source not in order[n + 1:i] else None
    return None


def program(nc, a, out):
    OPENING, BATCH, LAST = opening(), steps(), steps(after=False)
    opening_no, opening_total = numbered(OPENING)
    batch_no, batch_total = numbered(BATCH)
    last_no, _ = numbered(LAST)
    assert all(x["unit"] % 2 == 0 and x["turned"] % 2 == 0 for x in (opening_total, batch_total))

    def walk_batches(eng, walk):
        def parity(no):
            return lambda what, use: no[what][use] % 2

        walk(OPENING, 0, lambda what, use: opening_no[what][use], parity(opening_no))
        with eng.Fori(0, B - 1) as b:
            walk(BATCH, b, lambda what, use: b * batch_total[what] + (opening_total[what] + batch_no[what][use]),
                 parity(batch_no))
        walk(LAST, B - 1, lambda what, use: (B - 1) * batch_total[what] + opening_total[what] + last_no[what][use],
             parity(last_no))

    with ExitStack() as ctx:
        def sb(name, shape, dt=F32):
            return ctx.enter_context(nc.sbuf_tensor(name, shape, dt))

        def sem(name):
            return ctx.enter_context(nc.semaphore(name))

        ps = ctx.enter_context(nc.psum_tensor("ps", [P, 8 * BANK], F32))
        S_ps = ps[:, 0:4 * BANK]
        X_ps = ps[:, 3 * BANK:4 * BANK]
        T_ps = [ps[:, (4 + i) * BANK:(5 + i) * BANK] for i in range(2)]
        O_ps = ps[:, 6 * BANK:7 * BANK]
        M_ps = ps[:, 7 * BANK:8 * BANK]
        REL_OUT, PK_OUT = O_ps[:, 192:256], O_ps[:, 256:320]

        kfeat = sb("kfeat", [P, S])
        xt = [sb(f"xt{i}", [D, P + 1]) for i in range(2)]
        h0 = [sb(f"h0{i}", [P, D]) for i in range(2)]
        v1 = sb("v1", [P, NT, D])
        kT = sb("kT", [P, H2 // 2, S])
        v2 = sb("v2", [P, NT, H2, DH2])
        union = sb("union", [P, 16384])
        xin = [union[:, i * T * V:(i + 1) * T * V] for i in range(2)]
        rows = [union[:, r * 2048:(r + 1) * 2048].rearrange("p (s d) -> p s d", s=TOPK) for r in range(RING)]
        work = union[:, 8192:8192 + 4 * S]
        probs = [work[:, i * S:(i + 1) * S] for i in range(2)]
        probsT = [work[:, (2 + i) * S:(3 + i) * S] for i in range(2)]
        rot_prod = sb("rot_prod", [D, 4 * H1 * P])
        sim = sb("sim", [P, 2 * H2, NKEY])
        sim_rest = sb("sim_rest", [P, 2 * H2, NKEY])
        match = sb("match", [P, 2 * TOPK * NCAND])
        cand_rest = sb("cand_rest", [P, H2, NCAND])
        cand_i = sb("cand_i", [P, H2, NCAND])
        qfeat = union[:, 14336:15872]

        wq2 = sb("wq2", [D, P]); wk2 = sb("wk2", [D, P]); wv = sb("wv", [D, D]); wout = sb("wout", [D, D])
        wpos = sb("wpos", [D, 2, H1, D])
        bq2 = sb("bq2", [P, 1]); uv2 = sb("uv2", [P, 1]); bk2 = sb("bk2", [P, 1]); bquv = sb("bquv", [P, 1])
        bv = sb("bv", [P, D]); bout = sb("bout", [P, D]); gamma = sb("gamma", [P, D]); beta = sb("beta", [P, D])
        wqf = sb("wqf", [D, H2 * DH2]); wpk = sb("wpk", [D, 2 * H2 * DKEY]); wo = sb("wo", [P, H2 // 2, D])
        keys = sb("keys", [P, 4, 4 * NKEY])
        ident = sb("ident", [P, P]); rot = [sb(f"rot{i}", [D, 4, P]) for i in range(2)]
        upper = sb("upper", [P, P], I32); seam = sb("seam", [P, P + 1], I32); future = sb("future", [P, P])
        own = sb("own", [P, 3 * H1]); iota = sb("iota", [P, NCAND]); offs = sb("offs", [P, H2 * TOPK])
        dft = sb("dft", [2 * FREQ, PATCH]); wtok = sb("wtok", [P, PATCH // 2, D])
        w18 = kT[0:2 * FREQ, 0:3, :].rearrange("p a b -> p (a b)")[:, 0:C * D]
        wtok_p = v2[0:PATCH, :, :, :].rearrange("p a b c -> p (a b c)")[:, 0:C * D]

        h0s = kT[:, 0, 768:1536].rearrange("p (t d) -> p t d", t=NT)
        vst = kT[:, 1, 768:1536].rearrange("p (t d) -> p t d", t=NT)
        kst = kT[D:P, 2, :]
        txts = v2[:, 8:, :, :].rearrange("p a b c -> p (a b c)")[:, 0:B * 4 * D].rearrange("p (b t d) -> p b t d", b=B, t=4)
        ln_n = kT[:, 0, 0:768].rearrange("p (t d) -> p t d", t=NT)
        ln_q = kT[:, 1, 0:768].rearrange("p (t d) -> p t d", t=NT)
        xTs = kT[0:D, 2, :]
        embT = kT[0:D, 3, 0:NTOK * P]
        stat = sb("stat", [P, 6, NT])
        tl_n = sb("tl_n", [P, 1, D]); tl_q = sb("tl_q", [P, 1, D])
        qq = sb("qq", [P, P + 1])
        rowmax = sb("rowmax", [P, 2]); rowsum = sb("rowsum", [P, 2]); rowinv = sb("rowinv", [P, 2])
        ctx1 = sb("ctx1", [P, D]); ctxT = sb("ctxT", [D, P]); x2T = sb("x2T", [D, P])
        h1 = [sb(f"h1{i}", [P, D]) for i in range(4)]
        q2T = [sb(f"q2T{i}", [P, 4, P]) for i in range(4)]
        pkT = union[:, 15872:16384].rearrange("p (a b) -> p a b", a=4)
        best = sb("best", [P, 16, TOPK]); best_i = sb("best_i", [P, 16, TOPK], U32)
        i1s = sb("i1s", [P, H2, TOPK])
        cand = sb("cand", [P, H2, NCAND])
        fin = sb("fin", [P, H2, TOPK]); fin_pos = sb("fin_pos", [P, H2, TOPK], U32)
        picked = sb("picked", [P, 2 * TOPK])
        fsum = sb("fsum", [P, H2])
        weight = [sb(f"weight{i}", [P, H2, TOPK]) for i in range(2)]
        index = [sb(f"index{i}", [P, H2 * TOPK], U32) for i in range(2)]
        k2 = sb("k2", [P, H2 // 2, 2 * DH2])
        ao = sb("ao", [P, H2 * DH2]); aoT = sb("aoT", [P, 4, P])
        outt = [sb(f"outt{i}", [P, D]) for i in range(2)]

        weights_in = sem("weights_in"); consts_set = sem("consts_set")
        wtok_made = sem("wtok_made"); wtok_out = sem("wtok_out"); wtok_in = sem("wtok_in"); w18_used = sem("w18_used")
        bias_made = sem("bias_made")
        x_in = [sem(f"x_in{i}") for i in range(2)]; emb_made = sem("emb_made"); emb_kept = sem("emb_kept"); tok_made = sem("tok_made"); tok_kept = sem("tok_kept")
        ln_made = sem("ln_made"); xT_made = sem("xT_made"); xT_kept = sem("xT_kept"); xT_stored = sem("xT_stored"); h0_stored = sem("h0_stored"); k_stored = sem("k_stored"); v_stored = sem("v_stored")
        pad_stored = sem("pad_stored"); staged_free = sem("staged_free"); kv_in = sem("kv_in"); h0_used = sem("h0_used"); h0_in = [sem(f"h0_in{i}") for i in range(2)]; k_made = sem("k_made"); k_kept = sem("k_kept"); v_made = sem("v_made"); v_kept = sem("v_kept")
        scores_ready = sem("scores_ready")
        scores_free = sem("scores_free")
        max_ready = sem("max_ready")
        turned = sem("turned")
        turned_kept = sem("turned_kept")
        pv_ready = sem("pv_ready")
        misc_ready = sem("misc_ready")
        misc_kept = sem("misc_kept")
        feat_ready = sem("feat_ready")
        key_half = sem("key_half")
        rot_in = [sem(f"rot_in{i}") for i in range(2)]; xt_in = [sem(f"xt_in{i}") for i in range(2)]
        output_free = sem("output_free")
        rel_out = sem("rel_out"); x2_ready = sem("x2_ready")
        exp_asked = sem("exp_asked"); exp_made = sem("exp_made")
        index_ready = sem("index_ready")
        gathered = [sem(f"gathered{i}") for i in range(RING)]
        rows_free = sem("rows_free")
        k2_ready = sem("k2_ready"); pk_out = sem("pk_out")
        out_done = [sem(f"out_done{i}") for i in range(2)]

        xT_dram = nc.dram_tensor("xT_scratch", (D, B * S + 1), F32, kind="Internal").ap()
        h0_dram = nc.dram_tensor("h0_scratch", (B * S, D), F32, kind="Internal").ap()
        k_dram = nc.dram_tensor("k_scratch", (D, B * S), F32, kind="Internal").ap()
        v_dram = nc.dram_tensor("v_scratch", (B * S, D), F32, kind="Internal").ap()
        scratch = nc.dram_tensor("wtok_scratch", (PATCH, C, D), F32, kind="Internal").ap()
        small = [(wq2, "wq2"), (wk2, "wk2"), (wv, "wv"), (wout, "wout"), (wpos, "wpos"), (wqf, "wqf"), (wpk, "wpk"),
                 (bq2, "bq2"), (uv2, "uv2"), (bk2, "bk2"), (ident, "c_ident"), (upper, "c_upper"),
                 (seam, "c_seam"), (future, "c_future"), (own, "c_own"), (iota, "c_iota"), (offs, "c_offs"),
                 (dft, "c_dft")]
        rowwise = [(bv, "bv"), (bout, "bout"), (gamma, "gamma"), (beta, "beta")]
        N_LOADS = 1 + len(small) + len(rowwise) + 1 + 1 + B + 4

        passed = sem("passed")

        def stand(eng):
            eng.sem_inc(passed, 1)

        block = ctx.enter_context(nc.Block())

        @block.sync
        def _(sp):
            for s in out_done:
                sp.sem_inc(s, 16)
            sp.dma_start(w18, a["w18"]).then_inc(weights_in, 16)
            for dst, name in small:
                sp.dma_start(dst[:], a[name]).then_inc(weights_in, 16)
            for dst, name in rowwise:
                sp.dma_start(dst[:], a[name].partition_broadcast(P)).then_inc(weights_in, 16)
            sp.dma_start(wo[:], a["wo"].rearrange("(q p) d -> p q d", p=P)).then_inc(weights_in, 16)
            sp.dma_start(kfeat[0:D, :], a["c_pe"]).then_inc(weights_in, 16)
            for b in range(B):
                sp.dma_start(txts[:, b], a["txt"][b].rearrange("(t p) d -> p t d", p=P)).then_inc(weights_in, 16)
            sp.wait_ge(consts_set, 1)
            for q in range(4):
                sp.dma_start(keys[q * DKEY:(q + 1) * DKEY, :, q * NKEY:(q + 1) * NKEY],
                             a["keys"][:, q].rearrange("l d k -> d l k")).then_inc(weights_in, 16)
            sp.wait_ge(wtok_made, 1)
            sp.dma_start(scratch.rearrange("p c d -> p (c d)"), wtok_p).then_inc(wtok_out, 16)
            sp.wait_ge(wtok_out, 16)
            for half in range(2):
                sp.dma_start(wtok[half * C:(half + 1) * C, :, :],
                             scratch[half * 8:(half + 1) * 8].rearrange("p c d -> c p d")).then_inc(wtok_in, 16)
            with sp.Fori(0, B // 2) as i:
                for par in range(2):
                    sp.wait_ge(tok_made, i * 2 + par + 1)
                    x = a["x"][bass.ds(i * 2 + par, 1)].rearrange("b c t v -> (b c) (t v)")
                    sp.dma_start(xin[par][0:C, :], x).then_inc(x_in[par], 16)
                    sp.dma_start(xin[par][C:2 * C, 0:(T - STRIDE) * V], x[:, STRIDE * V:]).then_inc(x_in[par], 16)
                    pad = x[:, (T - 1) * V:].unsqueeze(1).broadcast_to([C, STRIDE, V])
                    sp.dma_start(xin[par][C:2 * C, (T - STRIDE) * V:].rearrange("c (t v) -> c t v", v=V),
                                 pad).then_inc(x_in[par], 16)

            for s in (xT_stored, h0_stored, k_stored, v_stored):
                sp.wait_ge(s, B * 16)
            sp.wait_ge(pad_stored, 16)

            def load_tile(b, t):
                i = t % 2
                if not (isinstance(b, int) and t < 2 and b == 0):
                    sp.wait_ge(feat_ready, b * NT + t + 1)
                    sp.wait_ge(h0_used, b * NT + t - 1)
                sp.dma_start(rot[i][:], a["c_rot"][t % NT]).then_inc(rot_in[i], 16)
                sp.dma_start(xt[i][:], xT_dram[:, bass.ds(b * S + t * P, P + 1)]).then_inc(xt_in[i], 16)
                sp.dma_start(h0[i][:], h0_dram[bass.ds(b * S + t * P, P), :]).then_inc(h0_in[i], 16)

            def load_batch(b):
                sp.dma_start(kfeat[D:P, :], k_dram[:, bass.ds(b * S, S)]).then_inc(kv_in, 16)
                sp.dma_start(v1[:], v_dram[bass.ds(b * S, S), :].rearrange("(t p) d -> p t d", p=P)).then_inc(kv_in, 16)

            def store_tile(b, t, at):
                sp.wait_ge(output_free, at("output", ("final", t)) + 2)
                sp.dma_start(out[bass.ds(b, 1), t * P:(t + 1) * P, :].rearrange("b p d -> (b p) d"),
                             outt[t % 2][:]).then_inc(out_done[t % 2], 16)

            def walk_sp(order, b, at, parity):
                if order is OPENING:
                    load_batch(0)
                    for t in range(4):
                        load_tile(0, t)
                    return
                for t in range(NT):
                    more = order is BATCH
                    if more or t + 4 < NT:
                        load_tile(b, t + 4)
                    if t == NT - 3 and more:
                        sp.wait_ge(pv_ready, at("unit", ("rel", NT - 1, H1 - 1)) + 3)
                        load_batch(b + 1)
                    if t > 1:
                        store_tile(b, t - 2, at)
                for t in (NT - 2, NT - 1):
                    store_tile(b, t, at)

            walk_batches(sp, walk_sp)
            for i in range(2):
                sp.wait_ge(out_done[i], 16 * (B * NT // 2) + 16)

        @block.gpsimd
        def _(pool):
            pool.wait_ge(consts_set, 1)
            pool.dma_start(xT_dram[:, B * S:B * S + 1], keys[0:D, 0, 200:201], allow_slow_non_contiguous=True).then_inc(pad_stored, 16)
            with pool.Fori(0, B) as b:
                pool.wait_ge(tok_kept, b + 2)
                pool.dma_start(h0_dram[bass.ds(b * S, S), :].rearrange("(t p) d -> p t d", p=P), h0s).then_inc(h0_stored, 16)
                pool.wait_ge(xT_kept, b + 1)
                pool.dma_start(xT_dram[:, bass.ds(b * S, S)], xTs).then_inc(xT_stored, 16)
                pool.wait_ge(k_kept, b + 2)
                pool.dma_start(k_dram[:, bass.ds(b * S, S)], kst).then_inc(k_stored, 16)
                pool.wait_ge(v_kept, b + 2)
                pool.dma_start(v_dram[bass.ds(b * S, S), :].rearrange("(t p) d -> p t d", p=P), vst).then_inc(v_stored, 16)
                for s in (h0_stored, xT_stored, k_stored, v_stored):
                    pool.wait_ge(s, b * 16 + 16)
                    stand(pool)
                pool.sem_inc(staged_free, 1)
            with pool.Fori(0, B) as b:
                for t in range(NT):
                    for h in range(H2):
                        n = t * H2 + h
                        if h % 2 == 0:
                            pool.wait_ge(index_ready, b * (NT * 4) + t * 4 + h // 2 + 1)
                            stand(pool)
                        pool.wait_ge(rows_free, b * (NT * H2) + n + 1)
                        stand(pool)
                        for s in range(TOPK):
                            pool.indirect_dma_start(
                                rows[n % RING][:, s, :], None, a["kv"],
                                bass.IndirectOffsetOnAxis(index[t % 2][:, h * TOPK + s:h * TOPK + s + 1], 0),
                            ).then_inc(gathered[n % RING], 16)

        @block.tensor
        def _(pe):
            pe.wait_ge(weights_in, 16 * N_LOADS)
            for c in range(C * D // BANK):
                last = pe.matmul(ps[0:PATCH, c * BANK:(c + 1) * BANK], dft[:], w18[:, c * BANK:(c + 1) * BANK],
                                 start=True, stop=True)
            last.then_inc(w18_used, 1)
            pe.wait_ge(wtok_made, 1)
            pe.wait_ge(wtok_in, 32)
            with pe.Fori(0, B // 2) as i:
                for par in range(2):
                    b = i * 2 + par
                    pe.wait_ge(x_in[par], i * 48 + 48)
                    pe.wait_ge(k_kept, b + 1)
                    pe.wait_ge(tok_kept, b + 1)
                    xv = xin[par].rearrange("k (n p v) -> k p v n", p=STRIDE, v=V)
                    vs = BANK // NPATCH
                    for p in range(STRIDE):
                        for k in range(V // vs):
                            last = pe.matmul(ps[0:D, k * BANK:(k + 1) * BANK], wtok[:, p, :], xv[:, p, k * vs:(k + 1) * vs, :],
                                             start=(p == 0), stop=(p == STRIDE - 1))
                    last.then_inc(emb_made, 1)
                    pe.wait_ge(emb_kept, b + 1)
                    stand(pe)
                    for k in range(NTOK):
                        last = pe.transpose(ps[:, k * D:(k + 1) * D], embT[:, k * P:(k + 1) * P], ident[0:D, 0:D])
                    last.then_inc(tok_made, 1)
                    pe.wait_ge(v_kept, b + 1)
                    pe.wait_ge(ln_made, b + 1)
                    stand(pe)
                    for k in range(NT):
                        last = pe.transpose(ps[0:D, (2 + k // 4) * BANK + (k % 4) * P:(2 + k // 4) * BANK + (k % 4 + 1) * P],
                                            ln_n[:, k, :], ident[:])
                    last.then_inc(xT_made, 1)
                    pe.wait_ge(xT_kept, b + 1)
                    for c in range(3):
                        last = pe.matmul(ps[:, (5 + c) * BANK:(6 + c) * BANK], wk2[:], xTs[:, c * BANK:(c + 1) * BANK],
                                         start=True, stop=True)
                    last.then_inc(k_made, 1)
                    for k in range(NT):
                        last = pe.matmul(ps[:, 2 * BANK + k * D:2 * BANK + (k + 1) * D], xTs[:, k * P:(k + 1) * P], wv[:],
                                         start=True, stop=True)
                    last.then_inc(v_made, 1)
            pe.wait_ge(k_kept, B + 1)
            pe.wait_ge(v_kept, B + 1)

            def walk_pe(order, b, at, parity):
                def misc_slot(use, ahead=0):
                    pe.wait_ge(misc_kept, at("misc", use) + 1 + ahead)

                def score_slot(step):
                    pe.wait_ge(scores_free, at("scores", step) + 1)

                def output_slot(step, ahead=0):
                    pe.wait_ge(output_free, at("output", step) + 1 + ahead)

                def fill_rot(step):
                    t = step[1]
                    misc_slot(("q", t), 1)
                    score_slot(step)
                    stand(pe)
                    for v in range(2):
                        for h in range(H1):
                            c = (v * H1 + h) * 2 * P
                            last = pe.matmul(S_ps[0:D, c:c + P + 1], wpos[:, v, h, :], qq[0:D, :], start=True, stop=True)
                    last.then_inc(scores_ready, 1)

                def fill_rel(step):
                    _, t, h = step
                    if h == 0:
                        pe.wait_ge(feat_ready, b * NT + t + 3)
                        pe.wait_ge(key_half, b * NT + t + 1)
                    t = t % NT
                    if h == 0 and t == 0:
                        pe.wait_ge(kv_in, b * 32 + (32 if order is OPENING else 64))
                    score_slot(step)
                    seam_at = (t + 1) * P
                    for kind, lo, hi in ((0, 0, seam_at), (1, seam_at, S)):
                        c = lo
                        while c < hi:
                            e = min(hi, (c // BANK + 1) * BANK)
                            q = (kind * H1 + h) * P
                            pe.matmul(S_ps[:, c:e], qfeat[:, q:q + P], kfeat[:, c:e], start=True, stop=True)
                            c = e
                    q = (H1 + h) * P
                    pe.matmul(X_ps[:, 0:P], qfeat[:, q:q + P], kfeat[:, t * P:(t + 1) * P], start=True, stop=True)
                    q = (2 * H1 + h) * P
                    w = P + 1 if t + 1 < NT else P
                    pe.matmul(X_ps[:, P:P + w], qfeat[:, q:q + P], kfeat[:, t * P:t * P + w],
                              start=True, stop=True).then_inc(scores_ready, 1)

                def fill_pk(step):
                    _, t, h = step
                    misc_slot(("kT", t, h // 2), 1)
                    score_slot(step)
                    p0 = (h % 2) * DH2
                    n = (t + 1) * P
                    for c in range(0, n, BANK):
                        e = min(n, c + BANK)
                        last = pe.matmul(S_ps[:, c:e], q2T[t % 4][p0:p0 + DH2, h // 2, :], kT[p0:p0 + DH2, h // 2, c:e],
                                         start=True, stop=True)
                    last.then_inc(scores_ready, 1)

                def fill_sim(step):
                    misc_slot(("pkT", step[1]), 1)
                    score_slot(step)
                    for q in range(4):
                        last = pe.matmul(S_ps[:, q * 4 * NKEY:(q + 1) * 4 * NKEY], pkT[:, q, :], keys[:, q, :],
                                         start=True, stop=True)
                    last.then_inc(scores_ready, 1)

                fill = {"rot": fill_rot, "rel": fill_rel, "pk": fill_pk, "sim": fill_sim}

                def turn(step):
                    tiles = tiles_of(step)
                    pe.wait_ge(scores_free, at("scores", step) + 2)
                    i = parity("unit", step)
                    for g in range(-(-tiles // 4)):
                        bank = T_ps[(parity("turned", step) + g) % 2]
                        pe.wait_ge(turned_kept, at("turned", step) + g + 1)
                        for j in range(4 * g, min(tiles, 4 * g + 4)):
                            last = pe.transpose(bank[:, (j % 4) * P:(j % 4 + 1) * P], probs[i][:, j * P:(j + 1) * P], ident[:])
                        last.then_inc(turned, 1)

                def weigh(step):
                    kind, t, h = step
                    tiles = tiles_of(step)
                    i = parity("unit", step)
                    output_slot(step)
                    for j in range(tiles):
                        if j % 4 == 0:
                            pe.wait_ge(turned_kept, at("turned", step) + j // 4 + 3)
                        if kind == "rel":
                            o, val = O_ps[:, h * DH1:(h + 1) * DH1], v1[:, j, h * DH1:(h + 1) * DH1]
                        else:
                            o, val = O_ps[:, D + i * DH2:D + (i + 1) * DH2], v2[:, j, h, :]
                        last = pe.matmul(o, probsT[i][:, j * P:(j + 1) * P], val, start=(j == 0), stop=(j == tiles - 1))
                    last.then_inc(pv_ready, 1)

                def queries(t):
                    pe.wait_ge(xt_in[t % 2], b * (NT // 2) * 16 + 16 * (t // 2) + 16)
                    misc_slot(("q", t))
                    pe.matmul(M_ps[:, 0:P + 1], wq2[:], xt[t % 2][:], start=True, stop=True).then_inc(misc_ready, 1)

                def project(t):
                    output_slot(("rel", t, H1 - 1), 1)
                    misc_slot(("ctxT", t))
                    stand(pe)
                    pe.transpose(M_ps[0:D, 0:P], ctx1[:], ident[:]).then_inc(misc_ready, 1)
                    misc_slot(("ctxT", t), 1)
                    output_slot(("project", t))
                    stand(pe)
                    pe.matmul(REL_OUT, ctxT[:], wout[:], start=True, stop=True).then_inc(rel_out, 1)

                def norm(t):
                    pe.wait_ge(x2_ready, b * NT + t + 1)
                    misc_slot(("xT", t))
                    stand(pe)
                    pe.transpose(M_ps[0:D, 0:P], tl_n[:, 0, :], ident[:]).then_inc(misc_ready, 1)
                    for use, w in ((("qT", t), wqf), (("pkT", t), wpk)):
                        misc_slot(use)
                        for q in range(4):
                            last = pe.matmul(M_ps[:, q * P:(q + 1) * P], w[:, q * P:(q + 1) * P], x2T[:],
                                             start=True, stop=True)
                        last.then_inc(misc_ready, 1)

                def turn_keys(t, pair):
                    pe.wait_ge(k2_ready, b * (NT * 4) + t * 4 + pair + 1)
                    misc_slot(("kT", t, pair))
                    pe.transpose(M_ps[:, 0:P], k2[:, pair, :], ident[:]).then_inc(misc_ready, 1)

                def final(t):
                    output_slot(("pk", t, H2 - 1), 1)
                    misc_slot(("oT", t))
                    for q in range(4):
                        last = pe.transpose(M_ps[:, q * P:(q + 1) * P], ao[:, q * P:(q + 1) * P], ident[:])
                    last.then_inc(misc_ready, 1)
                    misc_slot(("oT", t), 1)
                    output_slot(("final", t))
                    for q in range(4):
                        last = pe.matmul(PK_OUT, aoT[:, q, :], wo[:, q, :], start=(q == 0), stop=(q == 3))
                    last.then_inc(pk_out, 1)

                other = {"q": queries, "project": project, "norm": norm, "kT": turn_keys, "final": final}
                filled = None
                for n, step in enumerate(order):
                    if step[0] in fill:
                        if filled is None:
                            fill[step[0]](step)
                        filled = next_scores(order, n)
                        if filled:
                            fill[filled[0]](filled)
                        if step[0] in ("rel", "pk"):
                            turn(step)
                            weigh(step)
                    elif step[0] in other:
                        other[step[0]](*step[1:])

            walk_batches(pe, walk_pe)

        @block.scalar
        def _(act):
            act.sem_inc(scores_free, 1)
            act.sem_inc(turned_kept, 2)
            act.sem_inc(misc_kept, 1)
            act.sem_inc(tok_kept, 1)
            act.sem_inc(k_kept, 1)
            act.sem_inc(tok_made, 2)
            act.sem_inc(v_made, 1)
            act.sem_inc(xT_made, 1)
            act.sem_inc(staged_free, 1)
            act.wait_ge(w18_used, 1)
            act.activation(wtok_p[:, 0:2048], ps[0:PATCH, 0:2048], ACT.Copy)
            act.activation(wtok_p[:, 2048:4096], ps[0:PATCH, 2048:4096], ACT.Copy).then_inc(wtok_made, 1)
            with act.Fori(0, B) as b:
                act.wait_ge(emb_made, b + 1)
                act.activation(embT, ps[0:D, 0:NTOK * P], ACT.Copy).then_inc(emb_kept, 1)
                act.wait_ge(staged_free, b + 1)
                act.activation(h0s[:, NTOK:, :], txts[:, bass.ds(b, 1)].rearrange("p b t d -> p (b t) d"), ACT.Copy)
                act.wait_ge(tok_made, b + 3)
                act.activation(h0s[:, 0:NTOK, :].rearrange("p t d -> p (t d)"), ps[:, 0:NTOK * D],
                               ACT.Copy).then_inc(tok_kept, 1)
                act.wait_ge(xT_made, b + 2)
                act.activation(xTs, ps[0:D, 2 * BANK:5 * BANK], ACT.Copy).then_inc(xT_kept, 1)
                act.wait_ge(k_made, b + 1)
                act.activation(kst, ps[D:P, 5 * BANK:8 * BANK], ACT.Identity,
                               bias=bk2[D:P, 0:1]).then_inc(k_kept, 1)

            def walk_act(order, b, at, parity):
                def copy_misc(use, dst, src, func=ACT.Copy, **kw):
                    act.wait_ge(misc_ready, at("misc", use) + 1)
                    act.activation(dst, src, func, **kw).then_inc(misc_kept, 1)

                def exps(step):
                    i, n = parity("unit", step), tiles_of(step) * P
                    act.wait_ge(max_ready, at("unit", step) + 1)
                    act.activation(probs[i][:, 0:n], S_ps[:, 0:n], ACT.Exp,
                                   bias=rowmax[:, i:i + 1], accum_out=rowsum[:, i:i + 1]).then_inc(scores_free, 1)

                def copy_turned(step):
                    i, tiles = parity("unit", step), tiles_of(step)
                    act.wait_ge(pv_ready, at("unit", step) + 1)
                    for g in range(-(-tiles // 4)):
                        bank = T_ps[(parity("turned", step) + g) % 2]
                        act.wait_ge(turned, at("turned", step) + g + 1)
                        w = min(tiles - 4 * g, 4) * P
                        act.activation(probsT[i][:, g * BANK:g * BANK + w], bank[:, 0:w], ACT.Copy).then_inc(turned_kept, 1)

                for step in order:
                    kind, t = step[:2]
                    if kind in ("rel", "pk"):
                        exps(step)
                        copy_turned(step)
                    elif kind == "q":
                        copy_misc(step, qq[:], M_ps[:, 0:P + 1], ACT.Identity, bias=bquv[:, 0:1])
                    elif kind == "project":
                        copy_misc(("ctxT", t), ctxT[:], M_ps[0:D, 0:P])
                    elif kind == "norm":
                        copy_misc(("xT", t), x2T[:], M_ps[0:D, 0:P])
                        copy_misc(("qT", t), q2T[t % 4][:].rearrange("p a b -> p (a b)"), M_ps, scale=DH2 ** -0.5)
                        copy_misc(("pkT", t), pkT.rearrange("p a b -> p (a b)"), M_ps)
                    elif kind == "rot":
                        act.wait_ge(scores_ready, at("scores", step) + 1)
                        stand(act)
                        for h in range(H1):
                            ins = act.activation(qfeat[D:P, :].rearrange("p (k h i) -> p k h i", k=3, h=H1)[:, :, h, :],
                                                 qq[D:P, 0:P].unsqueeze(1).broadcast_to([D, 3, P]), ACT.Copy,
                                                 scale=own[D:P, h:h + 1])
                        ins.then_inc(key_half, 1)
                    elif kind == "sim":
                        act.wait_ge(scores_ready, at("scores", step) + 1)
                        act.activation(sim[:].rearrange("p l k -> p (l k)"), S_ps[:, 0:1024], ACT.Copy).then_inc(scores_free, 1)
                    elif kind == "select" and step[2] == 3:
                        act.wait_ge(exp_asked, b * NT + t + 1)
                        act.activation(fin[:], fin[:], ACT.Exp).then_inc(exp_made, 1)
                    elif kind == "kT":
                        copy_misc(step, kT[:, step[2], t % NT * P:(t % NT + 1) * P], M_ps[:, 0:P])
                    elif kind == "final":
                        copy_misc(("oT", t), aoT[:].rearrange("p a b -> p (a b)"), M_ps)

            walk_batches(act, walk_act)

        @block.vector
        def _(dve):
            stat_bits = stat[:].bitcast(I32)

            def layer_norm(src, dst, sq, n):
                mean, ssum, var, inv, tmp = (stat[:, k, 0:n] for k in (0, 1, 2, 4, 5))
                half = stat_bits[:, 3, 0:n]
                dve.tensor_reduce(ssum, src, AX.X, ALU.add)
                dve.drain()
                dve.tensor_scalar(mean, ssum, 1.0 / D, None, ALU.mult)
                dve.drain()
                dve.tensor_tensor(dst, src, mean.unsqueeze(2).broadcast_to([P, n, D]), ALU.subtract)
                dve.drain()
                dve.tensor_tensor(sq, dst, dst, ALU.mult)
                dve.drain()
                dve.tensor_reduce(ssum, sq, AX.X, ALU.add)
                dve.drain()
                dve.tensor_scalar(var, ssum, 1.0 / D, EPS, ALU.mult, ALU.add)
                dve.drain()
                dve.tensor_scalar(half, stat_bits[:, 2, 0:n], 1, None, ALU.logical_shift_right)
                dve.drain()
                dve.tensor_scalar(stat_bits[:, 4, 0:n], half, -1.0, float(0x5f3759df), ALU.mult, ALU.add)
                dve.drain()
                for _ in range(3):
                    dve.tensor_tensor(tmp, inv, inv, ALU.mult)
                    dve.drain()
                    dve.tensor_tensor(tmp, tmp, var, ALU.mult)
                    dve.drain()
                    dve.tensor_scalar(tmp, tmp, -0.5, 1.5, ALU.mult, ALU.add)
                    dve.drain()
                    dve.tensor_tensor(inv, inv, tmp, ALU.mult)
                    dve.drain()
                dve.tensor_tensor(dst, dst, inv.unsqueeze(2).broadcast_to([P, n, D]), ALU.mult)
                dve.drain()

            dve.memset(keys[:], 0.0).then_inc(consts_set, 1)
            dve.sem_inc(v_kept, 1)
            dve.sem_inc(feat_ready, 2)
            dve.sem_inc(pv_ready, 2)
            dve.sem_inc(output_free, 1)
            dve.sem_inc(rows_free, RING)
            dve.wait_ge(weights_in, 16 * N_LOADS)
            dve.tensor_tensor(bquv[:], bq2[:], uv2[:], ALU.add).then_inc(bias_made, 1)
            with dve.Fori(0, B) as b:
                dve.wait_ge(tok_kept, b + 2)
                dve.wait_ge(xT_made, b + 1)
                layer_norm(h0s, ln_n, ln_q, NT)
                layer_norm(ln_n, ln_n, ln_q, NT)
                dve.tensor_tensor(ln_n, ln_n, gamma[:].unsqueeze(1).broadcast_to([P, NT, D]), ALU.mult)
                dve.drain()
                dve.tensor_tensor(ln_n, ln_n, beta[:].unsqueeze(1).broadcast_to([P, NT, D]), ALU.add).then_inc(ln_made, 1)
                dve.wait_ge(v_made, b + 2)
                dve.tensor_tensor(vst,
                                  ps[:, 2 * BANK:2 * BANK + NT * D].rearrange("p (t d) -> p t d", t=NT),
                                  bv[:].unsqueeze(1).broadcast_to([P, NT, D]), ALU.add).then_inc(v_kept, 1)

            dve.memset(qfeat[0:D, 2 * H1 * P:3 * H1 * P], 0.0)
            def walk_dve(order, b, at, parity):
                def features(t):
                    dve.wait_ge(misc_kept, at("misc", ("q", t)) + 2)
                    dve.wait_ge(scores_ready, at("scores", ("rot", t)) + 1)
                    dve.wait_ge(rot_in[t % 2], b * (NT // 2) * 16 + 16 * (t // 2) + 16)
                    for kind in range(2):
                        ins = dve.tensor_tensor(
                            rot_prod[:, kind * 2 * H1 * P:(kind + 1) * 2 * H1 * P].rearrange("p (v h i) -> p v h i", v=2, h=H1),
                            S_ps[0:D, :].rearrange("p (v h i) -> p v h i", v=2, h=H1)[:, :, :, kind:kind + P],
                            rot[t % 2][:, 2 * kind:2 * kind + 2, :].unsqueeze(2).broadcast_to([D, 2, H1, P]), ALU.mult)
                    ins.then_inc(scores_free, 1)
                    dve.drain()
                    r = rot_prod[:].rearrange("p (k v n) -> p k v n", k=2, v=2)
                    dve.tensor_tensor(qfeat[0:D, 0:2 * H1 * P].rearrange("p (k n) -> p k n", k=2),
                                      r[:, :, 0, :], r[:, :, 1, :], ALU.add).then_inc(feat_ready, 1)

                def rel_max(t, h):
                    key = ("rel", t, h)
                    par = parity("unit", key)
                    dve.wait_ge(scores_ready, at("scores", key) + 1)
                    t = t % NT
                    stand(dve)
                    dve.copy_predicated(S_ps[:, t * P:(t + 1) * P], upper[:], X_ps[:, 0:P])
                    dve.drain()
                    w = P + 1 if t + 1 < NT else P
                    dve.copy_predicated(S_ps[:, t * P:t * P + w], seam[:, 0:w], X_ps[:, P:P + w])
                    dve.drain()
                    dve.tensor_reduce(rowmax[:, par:par + 1], S_ps[:, 0:S], AX.X, ALU.max, negate=True).then_inc(max_ready, 1)

                def pk_max(t, h):
                    key = ("pk", t, h)
                    par = parity("unit", key)
                    dve.wait_ge(scores_ready, at("scores", key) + 1)
                    dve.tensor_tensor(S_ps[:, t * P:(t + 1) * P], S_ps[:, t * P:(t + 1) * P], future[:], ALU.add)
                    dve.drain()
                    dve.tensor_reduce(rowmax[:, par:par + 1], S_ps[:, 0:(t + 1) * P], AX.X, ALU.max,
                                      negate=True).then_inc(max_ready, 1)

                def normalise(key):
                    kind, t, h = key
                    par = parity("unit", key)
                    dve.wait_ge(pv_ready, at("unit", key) + 3)
                    dve.reciprocal(rowinv[:, par:par + 1], rowsum[:, par:par + 1])
                    dve.drain()
                    if kind == "rel":
                        ins = dve.tensor_scalar(ctx1[:, h * DH1:(h + 1) * DH1], O_ps[:, h * DH1:(h + 1) * DH1],
                                                rowinv[:, par:par + 1], None, ALU.mult)
                    else:
                        ins = dve.tensor_scalar(ao[:, h * DH2:(h + 1) * DH2], O_ps[:, D + par * DH2:D + (par + 1) * DH2],
                                                rowinv[:, par:par + 1], None, ALU.mult)
                    ins.then_inc(output_free, 1)

                def mix_rows(t, h):
                    n = t * H2 + h
                    g = rows[n % RING]
                    dve.wait_ge(gathered[n % RING], b * (NT * H2 // RING * TOPK * 16) + (n // RING + 1) * TOPK * 16)
                    dve.tensor_tensor(g, g, weight[t % 2][:, h, :].unsqueeze(2).broadcast_to([P, TOPK, 2 * DH2]), ALU.mult)
                    dve.drain()
                    gd = g.rearrange("p s d -> p d s")
                    dve.tensor_reduce(k2[:, h // 2, (h % 2) * DH2:(h % 2 + 1) * DH2], gd[:, 0:DH2, :], AX.X, ALU.add)
                    ins = dve.tensor_reduce(v2[:, t % NT, h, :], gd[:, DH2:2 * DH2, :], AX.X, ALU.add).then_inc(rows_free, 1)
                    if h % 2:
                        dve.drain().then_inc(k2_ready, 1)

                def after_attention(t):
                    dve.wait_ge(rel_out, b * NT + t + 1)
                    dve.tensor_tensor(tl_q[:, 0, :], REL_OUT, bout[:], ALU.add).then_inc(output_free, 1)
                    dve.drain()
                    dve.wait_ge(h0_in[t % 2], b * (NT // 2) * 16 + 16 * (t // 2) + 16)
                    dve.tensor_tensor(h1[t % 4][:], tl_q[:, 0, :], h0[t % 2][:], ALU.add).then_inc(h0_used, 1)
                    dve.drain()
                    layer_norm(h1[t % 4][:].unsqueeze(1), tl_n[:], tl_q[:], 1)
                    dve.drain().then_inc(x2_ready, 1)

                def select(t, part):
                    if part == 0:
                        dve.wait_ge(scores_free, at("scores", ("sim", t)) + 2)
                        stand(dve)
                        for l in range(2 * H2):
                            dve.max(best[:, l, 0:8], sim[:, l, :])
                        dve.drain()
                        for l in range(2 * H2):
                            dve.match_replace(sim_rest[:, l, :], best[:, l, 0:8], sim[:, l, :], LOWEST)
                            dve.max_index(best_i[:, l, 0:8], best[:, l, 0:8], sim[:, l, :])
                        dve.drain()
                    elif part == 1:
                        for l in range(2 * H2):
                            dve.max(best[:, l, 8:16], sim_rest[:, l, :])
                        dve.drain()
                        for l in range(2 * H2):
                            dve.max_index(best_i[:, l, 8:16], best[:, l, 8:16], sim_rest[:, l, :])
                        dve.drain()
                        dve.scalar_tensor_tensor(out=i1s[:].rearrange("p h r -> p (h r)"),
                                                 in0=best_i[:, H2:2 * H2, :].rearrange("p h r -> p (h r)"), scalar=float(NKEY),
                                                 in1=offs[:], op0=ALU.mult, op1=ALU.add)
                        dve.drain()
                    elif part == 2:
                        for c, first, second in ((cand, best[:, 0:H2, :], best[:, H2:2 * H2, :]),
                                                 (cand_i, best_i[:, 0:H2, :], i1s[:])):
                            done = 0
                            for r0, n in SPANS:
                                if n == 1:
                                    break
                                dve.tensor_tensor(c[:, :, done:done + n], second[:, :, 0:n],
                                                  first[:, :, r0:r0 + 1].broadcast_to([P, H2, n]), ALU.add)
                                done += n
                            dve.tensor_tensor(c[:, :, done:NCAND], first[:, :, r0:TOPK],
                                              second[:, :, 0:1].broadcast_to([P, H2, TOPK - r0]), ALU.add)
                        dve.drain()
                        for h in range(H2):
                            dve.max(fin[:, h, 0:8], cand[:, h, :])
                        dve.drain()
                        for h in range(H2):
                            dve.match_replace(cand_rest[:, h, :], fin[:, h, 0:8], cand[:, h, :], LOWEST)
                            dve.max_index(fin_pos[:, h, 0:8], fin[:, h, 0:8], cand[:, h, :])
                        dve.drain()
                    elif part == 3:
                        for h in range(H2):
                            dve.max(fin[:, h, 8:16], cand_rest[:, h, :])
                        dve.drain()
                        for h in range(H2):
                            dve.max_index(fin_pos[:, h, 8:16], fin[:, h, 8:16], cand_rest[:, h, :])
                        dve.drain()
                        dve.tensor_copy(fsum[:], fin[:, :, 0])
                        dve.drain()
                        dve.tensor_tensor(fin[:], fin[:], fsum[:].unsqueeze(2).broadcast_to([P, H2, TOPK]),
                                          ALU.subtract).then_inc(exp_asked, 1)
                    if part < 4:
                        return
                    q = part - 4
                    hs = slice(2 * q, 2 * q + 2)
                    m = match[:].rearrange("p (j c) -> p j c", c=NCAND)
                    dve.tensor_tensor(m, iota[:].unsqueeze(1).broadcast_to([P, 2 * TOPK, NCAND]),
                                      fin_pos[:, hs, :].rearrange("p h k -> p (h k)").unsqueeze(2)
                                      .broadcast_to([P, 2 * TOPK, NCAND]), ALU.is_equal)
                    dve.drain()
                    m4 = match[:].rearrange("p (h k c) -> p h k c", h=2, k=TOPK)
                    dve.tensor_tensor(m4, m4, cand_i[:, hs, :].unsqueeze(2).broadcast_to([P, 2, TOPK, NCAND]), ALU.mult)
                    dve.drain()
                    dve.tensor_reduce(picked[:], m, AX.X, ALU.add)
                    dve.drain()
                    dve.tensor_copy(index[t % 2][:, q * 2 * TOPK:(q + 1) * 2 * TOPK], picked[:]).then_inc(index_ready, 1)
                    if q < 3:
                        return
                    dve.wait_ge(exp_made, b * NT + t + 1)
                    dve.tensor_reduce(fsum[:], fin[:], AX.X, ALU.add)
                    dve.drain()
                    dve.reciprocal(fsum[:], fsum[:])
                    dve.drain()
                    dve.tensor_tensor(weight[t % 2][:], fin[:], fsum[:].unsqueeze(2).broadcast_to([P, H2, TOPK]), ALU.mult)
                    dve.drain()

                def store(t):
                    dve.wait_ge(pk_out, b * NT + t + 1)
                    dve.wait_ge(out_done[t % 2], b * (NT // 2) * 16 + 16 * (t // 2) + 16)
                    dve.tensor_tensor(outt[t % 2][:], PK_OUT, h1[t % 4][:], ALU.add).then_inc(output_free, 1)

                other = {"rot": features, "ln": after_attention, "mix": mix_rows, "select": select, "store": store}
                waiting = []
                for step in order:
                    if step[0] in ("rel", "pk", "rot") and len(waiting) > 1:
                        normalise(waiting.pop(0))
                    if step[0] in ("rel", "pk"):
                        (rel_max if step[0] == "rel" else pk_max)(*step[1:])
                        waiting.append(step)
                    elif step[0] in ("project", "final"):
                        while waiting:
                            normalise(waiting.pop(0))
                    elif step[0] in other:
                        other[step[0]](*step[1:])
                while waiting:
                    normalise(waiting.pop(0))

            walk_batches(dve, walk_dve)


def kernel(**inputs):
    import concourse.bacc as bacc
    from concourse.bass_utils import run_bass_kernel_spmd

    i = {k: np.asarray(v) for k, v in inputs.items()}
    wpos = i["L0_attn_Wpos"]
    turned = wpos.T.reshape(H1, DH1, D)
    folded = np.zeros((D, 2, H1, D), np.float32)
    for h in range(H1):
        folded[h * DH1:(h + 1) * DH1, 0, h] = np.concatenate([turned[h][:, 0::2], turned[h][:, 1::2]], 1)
        folded[h * DH1:(h + 1) * DH1, 1, h] = np.concatenate([turned[h][:, 1::2], turned[h][:, 0::2]], 1)
    bq, u, v = i["L0_attn_bq"], i["L0_attn_u_bias"].reshape(-1), i["L0_attn_v_bias"].reshape(-1)
    bk = i["L0_attn_bk"]
    arrays = {
        "x": i["x"], "txt": i["txt"],
        "w18": i["L0_tok_W"].reshape(D, 2 * FREQ, C).transpose(1, 2, 0).reshape(2 * FREQ, C * D),
        "wq2": np.concatenate([i["L0_attn_Wq"]] * 2, 1), "wk2": np.concatenate([i["L0_attn_Wk"]] * 2, 1),
        "wv": i["L0_attn_Wv"], "wout": i["L0_attn_Wout"], "wpos": folded,
        "bq2": np.concatenate([bq, bq])[:, None], "uv2": np.concatenate([v, u])[:, None],
        "bk2": np.concatenate([bk, bk])[:, None],
        "bv": i["L0_attn_bv"], "bout": i["L0_attn_bout"], "gamma": i["L0_attn_ln_gamma"], "beta": i["L0_attn_ln_beta"],
        "wqf": i["L0_ffn_Wq"], "wpk": i["L0_ffn_Wq_pk"], "wo": i["L0_ffn_Wo"],
        "keys": i["L0_ffn_pk_keys"].transpose(0, 2, 3, 1).reshape(4, 4, DKEY, NKEY),
        "kv": np.concatenate([i["L0_ffn_keys_table"], i["L0_ffn_values_table"]], 1),
        **shape_constants(),
    }
    arrays = {k: np.ascontiguousarray(v) for k, v in arrays.items()}
    nc = bacc.Bacc("TRN2", target_bir_lowering=False, num_devices=1)
    nc.disable_value_cache = True
    aps = {k: nc.dram_tensor(f"in_{k}", v.shape, mybir.dt.from_np(v.dtype), kind="ExternalInput").ap()
           for k, v in arrays.items()}
    out = nc.dram_tensor("out_0", (B, S, D), F32, kind="ExternalOutput").ap()
    program(nc, aps, out)
    r = run_bass_kernel_spmd(nc, [{f"in_{k}": v for k, v in arrays.items()}], core_ids=[0])
    return r.results[0]["out_0"]
```
